# Optimizing a Trainium2 kernel written in Bass

```python
import numpy as np
import jax
import jax.numpy as jnp

def _softmax(x, axis=-1):
    return jax.nn.softmax(x, axis=axis)

def _gelu(x):
    return jax.nn.gelu(x, approximate=True)

def _silu(x):
    return jax.nn.silu(x)

def _sigmoid(x):
    return jax.nn.sigmoid(x)

def _layernorm(x, axis=-1, eps=1e-05):
    m = jnp.mean(x, axis=axis, keepdims=True)
    v = jnp.var(x, axis=axis, keepdims=True)
    return (x - m) / jnp.sqrt(v + eps)

def _scatter_add(tgt, idx, src, axis=0):
    return tgt.at[idx].add(src)

def _segment_sum(src, seg, n):
    return jax.ops.segment_sum(src, seg, n)
kernel_name = 'mk_gnn_resnorm_d2_gnn_r64_6d0bc6'

def setup_inputs(seed: int=0):
    np.random.seed(seed)
    _w = jnp.asarray

    def _rec_inputs():
        import jax
        import jax.numpy as jnp
        _gk = jax.random.key(seed)
        x = -0.0002928 + 1 * jax.random.normal(jax.random.fold_in(_gk, 1), (100000, 64), jnp.float32)
        src = jax.random.randint(jax.random.fold_in(_gk, 2), (25000,), 0, 100000, jnp.int32)
        dst = jax.random.randint(jax.random.fold_in(_gk, 3), (25000,), 0, 100000, jnp.int32)
        _o = jnp.argsort(dst, stable=True)
        src = src[_o]
        dst = dst[_o]
        edge_attr_32 = 0.000189758 + 1.00013 * jax.random.normal(jax.random.fold_in(_gk, 11), (25000, 32), jnp.float32)
        edge_weight = jax.random.uniform(jax.random.fold_in(_gk, 13), (25000,), jnp.float32, 0.0, 0.999999)
        edge_weight_n2 = jax.random.uniform(jax.random.fold_in(_gk, 14), (25000,), jnp.float32, 0.0, 0.999999)
        return (x, src, dst, edge_attr_32, edge_weight, edge_weight_n2)
    x, src, dst, edge_attr_32, edge_weight, edge_weight_n2 = _rec_inputs()

    def _L0_gnn_setup():
        import jax, jax.numpy as jnp
        import numpy as np
        N, E, D_IN, D_OUT = (1024, 16384, 64, 64)
        EPS = 1e-08
        key = jax.random.key(seed)
        ks = jax.random.split(key, 8)
        h = jax.random.normal(ks[0], (N, D_IN), dtype=jnp.float32)
        edge_index = jax.random.randint(ks[1], (2, E), 0, N, dtype=jnp.int64 if jax.config.jax_enable_x64 else jnp.int32)
        adj_v = jax.random.uniform(ks[2], (E,), dtype=jnp.float32)
        deg_v = jax.random.uniform(ks[3], (E,), dtype=jnp.float32)
        W = jax.random.normal(ks[4], (D_IN, D_OUT), dtype=jnp.float32) / np.sqrt(D_IN)
        b = jax.random.normal(ks[5], (D_OUT,), dtype=jnp.float32) * 0.01
        deg_coeff = jnp.array([0.5, 0.0], dtype=jnp.float32)
        coeff_param = jnp.zeros((3,), dtype=jnp.float32)
        scale_param = 2.0 * jnp.ones((1,), dtype=jnp.float32)
        return {'h': h, 'edge_index': edge_index, 'adj_v': adj_v, 'deg_v': deg_v, 'W': W, 'b': b, 'deg_coeff': deg_coeff, 'coeff_param': coeff_param, 'scale_param': scale_param}
    _L0_gnn_all = _L0_gnn_setup()
    _L0_gnn_in = {k: v for k, v in _L0_gnn_all.items() if k in ('W', 'b', 'deg_coeff', 'coeff_param', 'scale_param')}
    del _L0_gnn_all

    def _L1_gnn_setup():
        import jax, jax.numpy as jnp
        import numpy as np
        N_NODES = 100000
        N_EDGES = 25000
        NODE_DIM = 64
        EDGE_DIM = 32
        HIDDEN = 64
        key = jax.random.key(seed)
        ks = jax.random.split(key, 12)

        def lin(k, out_d, in_d):
            bound = 1.0 / np.sqrt(in_d)
            kw, kb = jax.random.split(k)
            W = jax.random.uniform(kw, (out_d, in_d), jnp.float32, -bound, bound)
            b = jax.random.uniform(kb, (out_d,), jnp.float32, -bound, bound)
            return (W, b)
        x = jax.random.normal(ks[0], (N_NODES, NODE_DIM), jnp.float32)
        edge_index = jax.random.randint(ks[1], (2, N_EDGES), 0, N_NODES, jnp.int64)
        edge_feat = jax.random.normal(ks[2], (N_EDGES, EDGE_DIM), jnp.float32)
        We1, be1 = lin(ks[3], HIDDEN, NODE_DIM * 2 + EDGE_DIM)
        We2, be2 = lin(ks[4], HIDDEN, HIDDEN)
        Wn1, bn1 = lin(ks[5], HIDDEN, NODE_DIM + HIDDEN)
        Wn2, bn2 = lin(ks[6], HIDDEN, HIDDEN)
        return {'x': x, 'edge_index': edge_index, 'edge_feat': edge_feat, 'We1': We1, 'be1': be1, 'We2': We2, 'be2': be2, 'Wn1': Wn1, 'bn1': bn1, 'Wn2': Wn2, 'bn2': bn2}
    _L1_gnn_all = _L1_gnn_setup()
    _L1_gnn_in = {k: v for k, v in _L1_gnn_all.items() if k in ('We1', 'be1', 'We2', 'be2', 'Wn1', 'bn1', 'Wn2', 'bn2')}
    del _L1_gnn_all
    return {'x': x, 'src': src, 'dst': dst, 'edge_attr_32': edge_attr_32, 'edge_weight': edge_weight, 'edge_weight_n2': edge_weight_n2, 'L0_gnn_W': _L0_gnn_in['W'], 'L0_gnn_b': _L0_gnn_in['b'], 'L0_gnn_deg_coeff': _L0_gnn_in['deg_coeff'], 'L0_gnn_coeff_param': _L0_gnn_in['coeff_param'], 'L0_gnn_scale_param': _L0_gnn_in['scale_param'], 'L1_gnn_We1': _L1_gnn_in['We1'], 'L1_gnn_be1': _L1_gnn_in['be1'], 'L1_gnn_We2': _L1_gnn_in['We2'], 'L1_gnn_be2': _L1_gnn_in['be2'], 'L1_gnn_Wn1': _L1_gnn_in['Wn1'], 'L1_gnn_bn1': _L1_gnn_in['bn1'], 'L1_gnn_Wn2': _L1_gnn_in['Wn2'], 'L1_gnn_bn2': _L1_gnn_in['bn2']}

def reference(x, src, dst, edge_attr_32, edge_weight, edge_weight_n2, L0_gnn_W, L0_gnn_b, L0_gnn_deg_coeff, L0_gnn_coeff_param, L0_gnn_scale_param, L1_gnn_We1, L1_gnn_be1, L1_gnn_We2, L1_gnn_be2, L1_gnn_Wn1, L1_gnn_bn1, L1_gnn_Wn2, L1_gnn_bn2):
    import jax
    import jax.numpy as jnp

    def _L0_gnn_ref(h, edge_index, adj_v, deg_v, W, b, deg_coeff, coeff_param, scale_param):
        import jax, jax.numpy as jnp
        import numpy as np
        N, E, D_IN, D_OUT = (1024, 16384, 64, 64)
        EPS = 1e-08
        n_nodes = h.shape[0]
        Wh = h @ W + b
        row, col = (edge_index[0], edge_index[1])
        sc = jax.nn.softplus(deg_coeff[0] * deg_v + deg_coeff[1])
        Wr = Wh[row]
        Wc = Wh[col]
        dot = jnp.sum(Wr * Wc, axis=-1)
        nr = jnp.sqrt(jnp.sum(Wr * Wr, axis=-1))
        nc = jnp.sqrt(jnp.sum(Wc * Wc, axis=-1))
        sim = dot / jnp.maximum(nr * nc, EPS)
        sim_pos = jax.nn.relu(sim)
        sim_neg = -jax.nn.relu(-sim)
        no_diag = (row != col).astype(Wh.dtype)
        base = adj_v * sc * no_diag
        prop_pos = jax.ops.segment_sum((base * sim_pos)[:, None] * Wc, row, num_segments=n_nodes)
        prop_neg = jax.ops.segment_sum((base * sim_neg)[:, None] * Wc, row, num_segments=n_nodes)
        coeff = jax.nn.softmax(coeff_param)
        scale = jax.nn.softplus(scale_param)
        return scale * (coeff[0] * prop_pos + coeff[1] * prop_neg + coeff[2] * Wh)

    def _L1_gnn_ref(x, edge_index, edge_feat, We1, be1, We2, be2, Wn1, bn1, Wn2, bn2):
        import jax, jax.numpy as jnp
        import numpy as np
        N_NODES = 100000
        N_EDGES = 25000
        NODE_DIM = 64
        EDGE_DIM = 32
        HIDDEN = 64
        row, col = (edge_index[0], edge_index[1])
        m_input = jnp.concatenate([x[row], x[col], edge_feat], axis=-1)
        h = jax.nn.silu(m_input @ We1.T + be1)
        m_ij = jax.nn.silu(h @ We2.T + be2)
        agg = jax.ops.segment_sum(m_ij, row, num_segments=x.shape[0])
        h2 = jax.nn.silu(jnp.concatenate([x, agg], axis=-1) @ Wn1.T + bn1)
        return h2 @ Wn2.T + bn2
    edge_index = jnp.stack([src, dst])
    x = _layernorm(x + _L0_gnn_ref(x, edge_index, edge_weight, edge_weight_n2, L0_gnn_W, L0_gnn_b, L0_gnn_deg_coeff, L0_gnn_coeff_param, L0_gnn_scale_param), axis=-1)
    x = _layernorm(x + _L1_gnn_ref(x, edge_index, edge_attr_32, L1_gnn_We1, L1_gnn_be1, L1_gnn_We2, L1_gnn_be2, L1_gnn_Wn1, L1_gnn_bn1, L1_gnn_Wn2, L1_gnn_bn2), axis=-1)
    return x

_drawn_inputs = setup_inputs


def setup_inputs(seed=0):
    import zlib

    import numpy as np

    out = dict(_drawn_inputs(seed))
    spreads = {'L0_gnn_coeff_param': (0.0, 0.1)}
    factors = {'edge_attr_32': 8.0,
     'edge_weight': 5.346,
     'edge_weight_n2': 8.0,
     'L0_gnn_b': 7.852,
     'L0_gnn_deg_coeff': 8.0,
     'L1_gnn_We1': 8.0,
     'L1_gnn_be1': 41.218,
     'L1_gnn_We2': 8.0,
     'L1_gnn_be2': 64.0,
     'L1_gnn_bn1': 3.562}
    for name, (base, spread) in spreads.items():
        noise = np.random.default_rng([zlib.crc32(name.encode()), seed]).standard_normal(out[name].shape)
        drawn = base * np.exp(spread * noise) if base else spread * noise
        out[name] = jnp.asarray(drawn.astype(out[name].dtype))
    for name, factor in factors.items():
        out[name] = (out[name] * factor).astype(out[name].dtype)
    return out
```

```python
import concourse.bass as bass
from concourse import mybir
from contextlib import ExitStack

F32 = mybir.dt.float32
I32 = mybir.dt.int32
ALU = mybir.AluOpType
ACT = mybir.ActivationFunctionType
AXX = mybir.AxisListType.X


class Chain:

    def __init__(self, eng, sem, start=0):
        self.eng, self.sem, self.start, self.n = eng, sem, start, 0

    def step(self, ins):
        ins.then_inc(self.sem, 1)
        self.n += 1
        self.eng.wait_ge(self.sem, self.start + self.n)
        self.eng.nop(nofuse=True)


def wait(eng, sem, value):
    eng.wait_ge(sem, value)
    eng.nop(nofuse=True)


def gnn(nc, x, src, dst, edge_attr, edge_w, edge_w2, W, b, deg_coeff, coeff_param, scale_param,
        We1, be1, We2, be2, Wn1, bn1, Wn2, bn2, out):
    N, F = x.shape
    E, EF = edge_attr.shape
    P = 128
    T = -(-E // P)
    G = 4
    GROUPS = T // G
    assert T == GROUPS * G
    FULL = E // T
    REST = E - FULL * T
    assert FULL == P - 1
    TRASH = N
    R = 8
    CH = P * R
    HALF = GROUPS
    B_STEP = -(-(N - CH - HALF * CH) // (HALF - 1))
    B0 = N - CH - (HALF - 1) * B_STEP
    assert B0 <= HALF * CH and B_STEP <= CH
    EPS_LN, EPS_SIM = 1e-5, 1e-8
    S1, S2, S3, S4, S5, S6 = (slice(k * P, (k + 1) * P) for k in range(6))

    sums = nc.dram_tensor("prop_sums", [N + P, F], F32, kind="Internal").ap()
    aggs = nc.dram_tensor("message_sums", [N + P, F], F32, kind="Internal").ap()
    src_rows = nc.dram_tensor("src_rows", [T, P], F32, kind="Internal").ap()

    ctx = ExitStack()
    with ctx:
        def sb(name, shape, dt=F32):
            return ctx.enter_context(nc.sbuf_tensor(name, shape, dt))

        def ps(name):
            return ctx.enter_context(nc.psum_tensor(name, [P, 512], F32))

        def sem(name):
            return ctx.enter_context(nc.semaphore(name))

        ident = sb("ident", [P, P])
        lower = sb("lower", [P, P])
        ones = sb("ones", [1, P])
        lane = sb("lane", [P, 1])
        stage = sb("stage", [P, 9, P])
        wt = sb("wt", [P, 9, P])
        w2x = sb("w2x", [P, F])
        wmean = sb("wmean", [P, 1])
        w2c = sb("w2c", [P, F])
        w2z = sb("w2z", [P, F])
        wh_w = sb("wh_w", [P, P])
        wc_w = sb("wc_w", [P, F])
        z_w = sb("z_w", [P, P])
        n2_w = sb("n2_w", [P, P])
        brow = sb("brow", [P, F])
        brow_c = sb("brow_c", [P, F])
        zrow = sb("zrow", [P, F])
        be2_row = sb("be2_row", [P, F])
        bn2_row = sb("bn2_row", [P, F])
        bn2_c = sb("bn2_c", [P, F])
        zrow8 = sb("zrow8", [1, R, F])
        n2row8 = sb("n2row8", [1, R, F])
        rmean = sb("rmean", [P, 3])
        be1_col = sb("be1_col", [F, 1])
        bn1_col = sb("bn1_col", [P, 1])
        par = sb("par", [P, 6])
        pe_ = sb("par_e", [P, 8])
        cs = sb("cs", [P, 3])
        src_i = sb("src_i", [P, T], I32)
        dst_i = sb("dst_i", [P, T], I32)
        src_f = sb("src_f", [P, T])
        dst_f = sb("dst_f", [P, T])
        base = sb("base", [P, T])
        ew = sb("ew", [P, T])
        ew2 = sb("ew2", [P, T])
        tmp_a = sb("tmp_a", [P, T])
        tmp_b = sb("tmp_b", [P, T])
        gat_idx = sb("gat_idx", [P, T, 2], I32)
        off_trash = sb("off_trash", [P, T])
        sct_idx = sb("sct_idx", [P, T], I32)
        ef = sb("ef", [P, T, EF])
        srct = sb("srct", [P, 2, P])
        y_all = sb("y_all", [P, T, 2 * F])
        gi = sb("gi", [P, G, 2], I32)
        si = sb("si", [P, G], I32)
        xg = sb("xg", [P, G, 2 * F])
        xt = sb("xt", [P, G * P])
        efg = sb("efg", [P, P])
        eft = sb("eft", [P, P])
        ht = sb("ht", [F, G * P])
        srcb = sb("srcb", [P, G, P])
        same = sb("same", [P, G, P])
        before = sb("before", [P, G, P])
        wh = sb("wh", [P, G, 2 * F])
        whc = sb("whc", [P, G, F])
        sq = sb("sq", [P, G, 2 * F])
        prod = sb("prod", [P, G, F])
        n2 = sb("n2", [P, G, 2])
        nn = sb("nn", [P, G])
        dot = sb("dot", [P, G])
        sc1 = sb("sc1", [P, G])
        sc2 = sb("sc2", [P, G])
        cnt = sb("cnt", [P, G])
        msg = sb("msg", [P, G, F])
        sm = sb("sm", [P, G, F])
        rs = sb("rs", [P, 2 * G])
        var = sb("var", [P, 2 * G])
        tmps = sb("tmps", [P, 2 * G])
        vard = sb("vard", [P, R])
        tmpd = sb("tmpd", [P, R])
        xd = sb("xd", [P, R * F])
        xdt = sb("xdt", [P, R * F])
        sqd = sb("sqd", [P, R * F])
        rsd = sb("rsd", [P, R])
        x1d = sb("x1d", [P, R * F])
        hd = sb("hd", [P, R * F])
        vd = sb("vd", [P, R * F])
        od = sb("od", [P, R * F])
        ZW = (N + P) * F // P
        ZC = next(c for c in range(16, 200) if ZW % c == 0)
        zero = sb("zero", [P, ZW // ZC])

        p_t, p_b, p_w, p_z, p_s, p_d, p_e, p_f = (ps(n) for n in
                                                  ("p_t", "p_b", "p_w", "p_z", "p_s", "p_d", "p_e", "p_f"))
        xdt_k = [xdt[:, s] for s in (S1, S2, S3, S4)]

        pads_set = sem("pads_set"); zero_set = sem("zero_set"); consts_set = sem("consts_set")
        edges_in = sem("edges_in"); weights_in = sem("weights_in"); params_in = sem("params_in")
        tables_zero = sem("tables_zero"); ef_in = sem("ef_in")
        wt_ps = sem("wt_ps"); wt_set = sem("wt_set"); weights_set = sem("weights_set")
        srct_ps = sem("srct_ps"); srct_set = sem("srct_set"); src_rows_out = sem("src_rows_out")
        exps = sem("exps"); exp_in = sem("exp_in"); idx_set = sem("idx_set"); src_f_set = sem("src_f_set")
        dve_chain = sem("dve_chain"); pool_chain = sem("pool_chain")
        xd_in = sem("xd_in"); xd_t = sem("xd_t"); xdt_set = sem("xdt_set"); zd_ps = sem("zd_ps")
        sqd_set = sem("sqd_set"); x1d_set = sem("x1d_set"); x1d_t = sem("x1d_t"); x1dt_set = sem("x1dt_set")
        hd_ps = sem("hd_ps"); hd_set = sem("hd_set"); od_ps = sem("od_ps"); vd_set = sem("vd_set")
        sqd2_set = sem("sqd2_set"); od_set = sem("od_set"); od_out = sem("od_out"); dense_chain = sem("dense_chain")
        a_xg = [sem(f"a_xg{j}") for j in range(G)]
        a_srcb = sem("a_srcb"); a_xt_ps = sem("a_xt_ps"); a_xt = sem("a_xt"); a_wh_ps = sem("a_wh_ps")
        a_wh = sem("a_wh"); a_sq = sem("a_sq"); a_y = sem("a_y"); a_msg = sem("a_msg"); a_sum_ps = sem("a_sum_ps")
        a_sum = sem("a_sum"); a_acc = sem("a_acc"); a_same = sem("a_same")
        a_chain = sem("a_chain"); a_idx = sem("a_idx"); a_pool = sem("a_pool")
        b_pg = [sem(f"b_pg{j}") for j in range(G)]
        b_ef = sem("b_ef"); b_srcb = sem("b_srcb"); b_v = sem("b_v"); b_sq = sem("b_sq"); b_x1 = sem("b_x1"); b_xt_ps = sem("b_xt_ps")
        b_xt = sem("b_xt"); b_h_ps = sem("b_h_ps"); b_h = sem("b_h"); b_m_ps = sem("b_m_ps"); b_m0 = sem("b_m0")
        b_m = sem("b_m"); b_same = sem("b_same"); b_sum_ps = sem("b_sum_ps"); b_sum = sem("b_sum"); b_acc = sem("b_acc")
        b_chain = sem("b_chain"); b_pool = sem("b_pool")
        c_ag = [sem(f"c_ag{j}") for j in range(G)]
        c_x1 = sem("c_x1"); c_xt_ps = sem("c_xt_ps"); c_xt = sem("c_xt"); c_h_ps = sem("c_h_ps"); c_h = sem("c_h")
        c_o_ps = sem("c_o_ps"); c_v = sem("c_v"); c_sq = sem("c_sq"); c_out = sem("c_out"); c_sct = sem("c_sct")
        c_chain = sem("c_chain"); c_pool = sem("c_pool")

        def per_edge(a):
            return a[0:FULL * T].rearrange("(p t) -> p t", t=T), a[FULL * T:E].rearrange("(a t) -> a t", a=1)

        def row(a, n=P):
            return a.rearrange("(a f) -> a f", a=1).to_broadcast([n, a.shape[0]])

        N_EDGE = 8
        N_WEIGHT = 22
        block = ctx.enter_context(nc.Block())

        @block.sync
        def _(sp):
            sp.wait_ge(pads_set, 1)
            for a, t in ((src, src_i), (dst, dst_i), (edge_w, ew), (edge_w2, ew2)):
                whole, rest = per_edge(a)
                sp.dma_start(t[0:FULL, :], whole).then_inc(edges_in, 16)
                sp.dma_start(t[FULL:P, 0:REST], rest).then_inc(edges_in, 16)
            sp.dma_start(par[:, 0:3], row(coeff_param)).then_inc(params_in, 16)
            sp.dma_start(par[:, 3:4], row(scale_param)).then_inc(params_in, 16)
            sp.dma_start(par[:, 4:6], row(deg_coeff)).then_inc(params_in, 16)
            loads = [(w2x[0:F, :], W), (w2x[F:P, :], W), (stage[0:F, 0, :], We1[:, 0:P])]
            loads += [(stage[0:F, 1 + j, EF * j:EF * (j + 1)], We1[:, P:P + EF]) for j in range(G)]
            loads += [(stage[0:F, 5, 0:F], We2), (stage[0:F, 6, :], Wn1),
                      (stage[0:F, 7, 0:F], Wn1[:, 0:F]), (stage[F:P, 7, F:P], Wn1[:, 0:F]),
                      (stage[0:F, 8, 0:F], Wn2), (stage[F:P, 8, F:P], Wn2),
                      (brow[:, :], row(b)), (be2_row[:, :], row(be2)), (bn2_row[:, :], row(bn2)),
                      (be1_col[:, :], be1.rearrange("(f a) -> f a", a=1)),
                      (bn1_col[0:F, :], bn1.rearrange("(f a) -> f a", a=1)),
                      (bn1_col[F:P, :], bn1.rearrange("(f a) -> f a", a=1))]
            sp.wait_ge(zero_set, 2)
            for to, of in loads:
                sp.dma_start(to, of).then_inc(weights_in, 16)
            assert len(loads) == N_WEIGHT - 3
            for table in (sums, aggs):
                sp.dma_start(table.rearrange("n f -> (n f)").rearrange("(p c w) -> p c w", p=P, c=ZC),
                             zero[:, :].unsqueeze(1).to_broadcast([P, ZC, ZW // ZC])).then_inc(tables_zero, 16)
            sp.dma_start(ef[0:FULL, :, :], edge_attr[0:FULL * T, :].rearrange("(p t) f -> p t f", t=T)).then_inc(ef_in, 16)
            sp.dma_start(ef[FULL:P, 0:REST, :], edge_attr[FULL * T:E, :].rearrange("(a t) f -> a t f", a=1)).then_inc(ef_in, 16)
            sp.wait_ge(srct_set, 1)
            sp.dma_start(src_rows[0:P, :], srct[:, 0, :]).then_inc(src_rows_out, 16)
            sp.dma_start(src_rows[P:T, :], srct[0:T - P, 1, :]).then_inc(src_rows_out, 16)
            sp.wait_ge(src_rows_out, 32)

            def chunk(a, r0):
                return a[bass.ds(r0, CH), :].rearrange("(p r) f -> p (r f)", r=R)

            def load_srcb(i, sem_in):
                sp.dma_start(srcb[:, :, :].rearrange("p g e -> p (g e)"),
                             src_rows[bass.ds(i * G, G), :].rearrange("(a g) e -> a (g e)", a=1)
                             .to_broadcast([P, G * P])).then_inc(sem_in, 16)

            def store(d, r0):
                wait(sp, od_set, d + 1)
                sp.dma_start(chunk(out, r0), od[:, :]).then_inc(od_out, 16)

            sp.dma_start(xd[:, :], chunk(x, 0)).then_inc(xd_in, 16)
            with sp.Fori(0, HALF) as i:
                wait(sp, a_same, i)
                load_srcb(i, a_srcb)
                wait(sp, xd_t, i + 1)
                sp.dma_start(xd[:, :], chunk(x, (i + 1) * CH)).then_inc(xd_in, 16)
                store(i, i * CH)
                wait(sp, od_out, 16 * (i + 1))
            sp.wait_ge(xd_in, 16 * (HALF + 1))
            sp.dma_start(xd[:, :], chunk(x, B0)).then_inc(xd_in, 16)
            sp.wait_ge(a_same, GROUPS)
            with sp.Fori(0, HALF - 1) as i:
                wait(sp, b_same, i)
                load_srcb(i, b_srcb)
                wait(sp, xd_t, i + HALF + 1)
                sp.dma_start(xd[:, :], chunk(x, (i + 1) * B_STEP + B0)).then_inc(xd_in, 16)
                store(i + HALF, i * B_STEP + B0)
                wait(sp, od_out, 16 * (i + HALF + 1))
            sp.wait_ge(b_same, GROUPS - 1)
            load_srcb(GROUPS - 1, b_srcb)
            store(2 * HALF - 1, (HALF - 1) * B_STEP + B0)
            sp.wait_ge(od_out, 16 * 2 * HALF)

        @block.gpsimd
        def _(pool):
            ch = Chain(pool, pool_chain)
            ch.step(nc.gpsimd.memset(ident[:, :], 0.0))
            ch.step(nc.gpsimd.affine_select(out=ident[:, :], in_=ident[:, :], compare_op=ALU.not_equal, fill=1.0,
                                            base=0, pattern=[[-1, P]], channel_multiplier=1))
            ch.step(nc.gpsimd.memset(lower[:, :], 1.0))
            ch.step(nc.gpsimd.affine_select(out=lower[:, :], in_=lower[:, :], compare_op=ALU.is_gt, fill=0.0,
                                            base=0, pattern=[[-1, P]], channel_multiplier=1))
            ch.step(nc.gpsimd.iota(lane[:, :], pattern=[[0, 1]], base=N, channel_multiplier=1,
                                   allow_small_or_imprecise_dtypes=True))
            nc.gpsimd.memset(ones[:, :], 1.0).then_inc(consts_set, 1)

            def gather(to, table, index, done):
                nc.gpsimd.indirect_dma_start(to, None, table, bass.IndirectOffsetOnAxis(ap=index, axis=0))\
                    .then_inc(done, 16)

            def gathers(i, table, ready, free, done, halves, pool_sem, start):
                ch = Chain(pool, pool_sem, start)
                ch.step(nc.gpsimd.tensor_copy(gi[:, :, :], gat_idx[:, bass.ds(i * G, G), :]))
                wait(pool, free, i)
                for j in range(G):
                    for h in halves:
                        gather(xg[:, j, (h if len(halves) > 1 else 1) * F:(h if len(halves) > 1 else 1) * F + F],
                               table, gi[:, j, h:h + 1], done[j])

            def adds(i, table, ready, acc, pool_sem, start):
                ch = Chain(pool, pool_sem, start)
                wait(pool, acc, 16 * G * i)
                ch.step(nc.gpsimd.tensor_copy(si[:, :], sct_idx[:, bass.ds(i * G, G)]))
                wait(pool, ready, i + 1)
                for j in range(G):
                    wait(pool, acc, 16 * G * i + 16 * j)
                    nc.gpsimd.indirect_dma_start(table, bass.IndirectOffsetOnAxis(ap=si[:, j:j + 1], axis=0),
                                                 sm[:, j, :], None, compute_op=ALU.add).then_inc(acc, 16)

            pool.wait_ge(idx_set, 1)
            gathers(0, x, None, a_xt_ps, a_xg, (0, 1), a_pool, 0)
            pool.wait_ge(tables_zero, 32)
            with pool.Fori(0, GROUPS - 1) as i:
                for j in range(G):
                    wait(pool, a_xg[j], 32 * (i + 1))
                gathers(i + 1, x, None, a_xt_ps, a_xg, (0, 1), a_pool, i * 2 + 1)
                wait(pool, a_idx, i + 1)
                adds(i, sums, a_sum, a_acc, a_pool, i * 2 + 2)
            pool.wait_ge(a_idx, GROUPS)
            adds(GROUPS - 1, sums, a_sum, a_acc, a_pool, 2 * GROUPS - 1)
            pool.wait_ge(a_acc, 16 * T)
            for j in range(G):
                pool.wait_ge(a_xg[j], 32 * GROUPS)

            pool.wait_ge(a_xt_ps, GROUPS)
            gathers(0, sums, None, b_v, b_pg, (0, 1), b_pool, 0)
            with pool.Fori(0, GROUPS - 1) as i:
                for j in range(G):
                    wait(pool, b_pg[j], 32 * (i + 1))
                gathers(i + 1, sums, None, b_v, b_pg, (0, 1), b_pool, i * 2 + 1)
                adds(i, aggs, b_sum, b_acc, b_pool, i * 2 + 2)
            adds(GROUPS - 1, aggs, b_sum, b_acc, b_pool, 2 * GROUPS - 1)
            pool.wait_ge(b_acc, 16 * T)
            for j in range(G):
                pool.wait_ge(b_pg[j], 32 * GROUPS)

            def gathers_c(i, start):
                ch = Chain(pool, c_pool, start)
                ch.step(nc.gpsimd.tensor_copy(gi[:, :, :], gat_idx[:, bass.ds(i * G, G), :]))
                wait(pool, c_v, i)
                for j in range(G):
                    gather(xg[:, j, F:2 * F], aggs, gi[:, j, 0:1], c_ag[j])

            pool.wait_ge(b_v, GROUPS)
            gathers_c(0, 0)
            pool.wait_ge(od_out, 16 * 2 * HALF)
            with pool.Fori(0, GROUPS - 1) as i:
                for j in range(G):
                    wait(pool, c_ag[j], 16 * (i + 1))
                ch = Chain(pool, c_pool, i * 2 + 1)
                ch.step(nc.gpsimd.tensor_copy(gi[:, :, :], gat_idx[:, bass.ds((i + 1) * G, G), :]))
                wait(pool, c_v, i + 1)
                for j in range(G):
                    gather(xg[:, j, F:2 * F], aggs, gi[:, j, 0:1], c_ag[j])
                ch = Chain(pool, c_pool, i * 2 + 2)
                wait(pool, c_sct, 16 * G * i)
                ch.step(nc.gpsimd.tensor_copy(si[:, :], sct_idx[:, bass.ds(i * G, G)]))
                wait(pool, c_out, i + 1)
                for j in range(G):
                    wait(pool, c_sct, 16 * G * i + 16 * j)
                    nc.gpsimd.indirect_dma_start(out, bass.IndirectOffsetOnAxis(ap=si[:, j:j + 1], axis=0),
                                                 sm[:, j, :], None, bounds_check=N - 1, oob_is_err=False)\
                        .then_inc(c_sct, 16)
            scatters_last = GROUPS - 1
            ch = Chain(pool, c_pool, 2 * GROUPS - 1)
            pool.wait_ge(c_sct, 16 * G * (GROUPS - 1))
            ch.step(nc.gpsimd.tensor_copy(si[:, :], sct_idx[:, bass.ds(scatters_last * G, G)]))
            pool.wait_ge(c_out, GROUPS)
            for j in range(G):
                pool.wait_ge(c_sct, 16 * (G * scatters_last + j))
                nc.gpsimd.indirect_dma_start(out, bass.IndirectOffsetOnAxis(ap=si[:, j:j + 1], axis=0),
                                             sm[:, j, :], None, bounds_check=N - 1, oob_is_err=False)\
                    .then_inc(c_sct, 16)
            pool.wait_ge(c_sct, 16 * T)

        @block.tensor
        def _(pe):
            mm, tr = nc.tensor.matmul, nc.tensor.transpose

            pe.wait_ge(consts_set, 1)
            pe.wait_ge(src_f_set, 1)
            tr(p_t[:, 0:P], src_f[:, 0:P], ident[:, :])
            tr(p_t[0:T - P, P:2 * P], src_f[:, P:T], ident[:, :]).then_inc(srct_ps, 1)
            pe.wait_ge(weights_in, 16 * (N_WEIGHT - 3))
            for k in range(9):
                last = tr((p_w, p_z, p_s)[k // 4][:, (k % 4) * P:(k % 4 + 1) * P], stage[:, k, :], ident[:, :])
            last.then_inc(wt_ps, 1)
            pe.wait_ge(weights_set, 2)

            def dense_in(d):
                wait(pe, xd_in, xd_count(d))
                wait(pe, x1dt_set, d)
                for k in range(4):
                    last = tr(p_d[:, k * P:(k + 1) * P], xd[:, k * P:(k + 1) * P], ident[:, :])
                last.then_inc(xd_t, 1)

            def dense_z(d):
                wait(pe, xdt_set, d + 1)
                wait(pe, vd_set, d)
                for k in range(4):
                    mm(p_e[:, k * P:(k + 1) * P], xdt_k[k], z_w[:, :], start=True, stop=False)
                    last = mm(p_e[:, k * P:(k + 1) * P], ones[:, :],
                              zrow8[:, 2 * k:2 * k + 2, :].rearrange("a r f -> a (r f)"), start=False, stop=True)
                last.then_inc(zd_ps, 1)

            def dense_t(d):
                wait(pe, x1d_set, d + 1)
                for k in range(4):
                    last = tr(p_d[:, k * P:(k + 1) * P], x1d[:, k * P:(k + 1) * P], ident[:, :])
                last.then_inc(x1d_t, 1)

            def dense_h(d):
                wait(pe, x1dt_set, d + 1)
                mm(p_f[:, :], wt[:, 7, :], xdt[:, :], start=True, stop=True).then_inc(hd_ps, 1)

            def dense_o(d):
                wait(pe, hd_set, d + 1)
                for k in range(4):
                    mm(p_e[:, k * P:(k + 1) * P], hd[:, k * P:(k + 1) * P], n2_w[:, :], start=True, stop=False)
                    last = mm(p_e[:, k * P:(k + 1) * P], ones[:, :],
                              n2row8[:, 2 * k:2 * k + 2, :].rearrange("a r f -> a (r f)"), start=False, stop=True)
                last.then_inc(od_ps, 1)

            with pe.Fori(0, GROUPS) as i:
                xd_count = lambda d: 16 * d + 16
                dense_in(i)
                wait(pe, a_xt, i)
                for j in range(G):
                    wait(pe, a_xg[j], 32 * (i + 1))
                    last = tr(p_t[:, j * P:(j + 1) * P], xg[:, j, :], ident[:, :])
                last.then_inc(a_xt_ps, 1)
                dense_z(i)
                wait(pe, a_xt, i + 1)
                wait(pe, a_wh, i)
                wait(pe, a_y, i)
                for j in range(G):
                    lhs = xt[:, j * P:(j + 1) * P]
                    mm(p_w[:, j * P:(j + 1) * P], lhs, wh_w[:, :], start=True, stop=True)
                    mm(p_z[:, j * P:(j + 1) * P], lhs, z_w[:, :], start=True, stop=True)
                    last = mm(p_b[:, j * F:(j + 1) * F], lhs, wc_w[:, :], start=True, stop=True)
                last.then_inc(a_wh_ps, 1)
                dense_t(i)
                dense_h(i)
                wait(pe, a_msg, i + 1)
                wait(pe, a_same, i + 1)
                wait(pe, a_sum, i)
                for j in range(G):
                    last = mm(p_s[:, j * F:(j + 1) * F], same[:, j, :], msg[:, j, :], start=True, stop=True)
                last.then_inc(a_sum_ps, 1)
                dense_o(i)

            with pe.Fori(0, GROUPS) as i:
                xd_count = lambda d: 16 * d + 32
                dense_in(i + HALF)
                wait(pe, b_x1, i + 1)
                for j in range(G):
                    tr(p_t[:, j * P:(j + 1) * P], wh[:, j, :], ident[:, :])
                wait(pe, b_m0, i)
                wait(pe, b_ef, i + 1)
                tr(p_z[:, 0:P], efg[:, :], ident[:, :])\
                    .then_inc(b_xt_ps, 1)
                dense_z(i + HALF)
                wait(pe, b_xt, i + 1)
                for j in range(G):
                    s = slice(j * P, (j + 1) * P)
                    mm(p_w[0:F, s], wt[:, 0, 0:F], xt[:, s], start=True, stop=False)
                    last = mm(p_w[0:F, s], wt[:, 1 + j, 0:F], eft[:, :], start=False, stop=True)
                last.then_inc(b_h_ps, 1)
                dense_t(i + HALF)
                wait(pe, b_h, i + 1)
                for j in range(G):
                    last = mm(p_z[:, P + j * F:P + (j + 1) * F], ht[:, j * P:(j + 1) * P], wt[0:F, 5, 0:F],
                              start=True, stop=True)
                last.then_inc(b_m_ps, 1)
                dense_h(i + HALF)
                wait(pe, b_m, i + 1)
                wait(pe, b_same, i + 1)
                for j in range(G):
                    last = mm(p_s[:, j * F:(j + 1) * F], same[:, j, :], msg[:, j, :], start=True, stop=True)
                last.then_inc(b_sum_ps, 1)
                dense_o(i + HALF)

            with pe.Fori(0, GROUPS) as i:
                for j in range(G):
                    wait(pe, c_ag[j], 16 * (i + 1))
                wait(pe, c_x1, i + 1)
                wait(pe, c_xt, i)
                for j in range(G):
                    last = tr(p_t[:, j * P:(j + 1) * P], xg[:, j, :], ident[:, :])
                last.then_inc(c_xt_ps, 1)
                wait(pe, c_xt, i + 1)
                mm(p_w[0:F, :], wt[:, 6, 0:F], xt[:, :], start=True, stop=True).then_inc(c_h_ps, 1)
                wait(pe, c_h, i + 1)
                for j in range(G):
                    last = mm(p_z[:, j * F:(j + 1) * F], ht[:, j * P:(j + 1) * P], n2_w[0:F, 0:F],
                              start=True, stop=True)
                last.then_inc(c_o_ps, 1)

        @block.scalar
        def _(act):
            A = nc.scalar.activation
            act.wait_ge(exp_in, 1)
            A(pe_[:, 0:4], pe_[:, 0:4], ACT.Exp)
            A(tmp_a[:, :], tmp_a[:, :], ACT.Exp).then_inc(exps, 1)
            act.wait_ge(exps, 1)
            A(pe_[:, 3:4], pe_[:, 3:4], ACT.Ln, bias=1.0)
            A(tmp_a[:, :], tmp_a[:, :], ACT.Ln, bias=1.0).then_inc(exps, 1)
            act.wait_ge(srct_ps, 1)
            nc.scalar.copy(srct[:, 0, :], p_t[:, 0:P])
            nc.scalar.copy(srct[0:T - P, 1, :], p_t[0:T - P, P:2 * P]).then_inc(srct_set, 1)
            act.wait_ge(wt_ps, 1)
            nc.scalar.copy(wt[:, 0:4, :].rearrange("p k f -> p (k f)"), p_w[:, :])
            nc.scalar.copy(wt[:, 4:8, :].rearrange("p k f -> p (k f)"), p_z[:, :])
            nc.scalar.copy(wt[:, 8, :], p_s[:, 0:P]).then_inc(wt_set, 1)
            act.wait_ge(wt_set, 1)
            nc.scalar.copy(ht[0:1, 0:1], be1_col[0:1, :]).then_inc(weights_set, 1)

            def dense_xt(d):
                wait(act, xd_t, d + 1)
                wait(act, hd_ps, d)
                nc.scalar.copy(xdt[:, :], p_d[:, :]).then_inc(xdt_set, 1)

            def dense_sq(d):
                wait(act, zd_ps, d + 1)
                wait(act, od_set, d)
                A(sqd[:, :], p_e[:, :], ACT.Square).then_inc(sqd_set, 1)

            def dense_x1t(d):
                wait(act, x1d_t, d + 1)
                nc.scalar.copy(xdt[:, :], p_d[:, :]).then_inc(x1dt_set, 1)

            def dense_silu(d):
                wait(act, hd_ps, d + 1)
                wait(act, od_ps, d)
                A(hd[:, :], p_f[:, :], ACT.Silu, bias=bn1_col[:, :]).then_inc(hd_set, 1)

            def dense_sq2(d):
                wait(act, vd_set, d + 1)
                A(sqd[:, :], vd[:, :], ACT.Square).then_inc(sqd2_set, 1)

            with act.Fori(0, GROUPS) as i:
                dense_xt(i)
                wait(act, a_xt_ps, i + 1)
                wait(act, a_wh_ps, i)
                nc.scalar.copy(xt[:, :], p_t[:, :]).then_inc(a_xt, 1)
                dense_sq(i)
                wait(act, a_wh, i + 1)
                A(sq[:, :, :], wh[:, :, :], ACT.Square).then_inc(a_sq, 1)
                dense_x1t(i)
                dense_silu(i)
                wait(act, a_sum_ps, i + 1)
                wait(act, a_acc, 16 * G * i)
                nc.scalar.copy(sm[:, :, :].rearrange("p g f -> p (g f)"), p_s[:, 0:G * F]).then_inc(a_sum, 1)
                dense_sq2(i)

            act.wait_ge(a_acc, 16 * T)
            with act.Fori(0, GROUPS) as i:
                wait(act, b_xt_ps, i)
                nc.scalar.copy(efg[:, :], ef[:, bass.ds(i * G, G), :].rearrange("p g f -> p (g f)"))\
                    .then_inc(b_ef, 1)
                wait(act, b_v, i + 1)
                A(sq[:, :, :], wh[:, :, :], ACT.Square).then_inc(b_sq, 1)
                dense_xt(i + HALF)
                wait(act, b_xt_ps, i + 1)
                nc.scalar.copy(xt[:, :], p_t[:, :])
                nc.scalar.copy(eft[:, :], p_z[:, 0:P]).then_inc(b_xt, 1)
                nc.scalar.copy(y_all[:, bass.ds(i * G, G), 0:F], wh[:, :, 0:F])
                dense_sq(i + HALF)
                wait(act, b_h_ps, i + 1)
                A(ht[:, :], p_w[0:F, :], ACT.Silu, bias=be1_col[:, :]).then_inc(b_h, 1)
                dense_x1t(i + HALF)
                wait(act, b_m0, i + 1)
                A(msg[:, :, :], prod[:, :, :], ACT.Silu).then_inc(b_m, 1)
                dense_silu(i + HALF)
                wait(act, b_sum_ps, i + 1)
                wait(act, b_acc, 16 * G * i)
                nc.scalar.copy(sm[:, :, :].rearrange("p g f -> p (g f)"), p_s[:, 0:G * F]).then_inc(b_sum, 1)
                dense_sq2(i + HALF)

            with act.Fori(0, GROUPS) as i:
                wait(act, c_v, i)
                nc.scalar.copy(xg[:, :, 0:F], y_all[:, bass.ds(i * G, G), 0:F]).then_inc(c_x1, 1)
                wait(act, c_xt_ps, i + 1)
                nc.scalar.copy(xt[:, :], p_t[:, :]).then_inc(c_xt, 1)
                wait(act, c_h_ps, i + 1)
                A(ht[:, :], p_w[0:F, :], ACT.Silu, bias=bn1_col[0:F, :]).then_inc(c_h, 1)
                wait(act, c_v, i + 1)
                A(sq[:, :, 0:F], wh[:, :, 0:F], ACT.Square).then_inc(c_sq, 1)

        @block.vector
        def _(dve):
            V = nc.vector
            TT, TS, STT = V.tensor_tensor, V.tensor_scalar, V.scalar_tensor_tensor
            V.memset(src_i[96:P, :], N + P - 1)
            V.memset(dst_i[96:P, :], 0)
            V.memset(ew[96:P, :], 0.0)
            V.memset(ew2[96:P, :], 0.0).then_inc(pads_set, 1)
            V.memset(ef[96:P, :, :], 0.0).then_inc(zero_set, 1)
            V.memset(zero[:, :], 0.0)
            V.memset(stage[:, :, :], 0.0).then_inc(zero_set, 1)
            ch = Chain(dve, dve_chain)
            ch.step(V.memset(wh_w[:, :], 0.0))
            ch.step(V.memset(z_w[:, :], 0.0))
            ch.step(V.memset(wc_w[:, :], 0.0))
            ch.step(V.memset(n2_w[:, :], 0.0))
            dve.wait_ge(consts_set, 1)
            dve.wait_ge(edges_in, 16 * N_EDGE)
            V.tensor_copy(src_f[:, :], src_i[:, :]).then_inc(src_f_set, 1)
            dve.wait_ge(src_f_set, 1)
            ch.step(V.tensor_copy(dst_f[:, :], dst_i[:, :]))
            TS(gat_idx[:, :, 0], src_f[:, :], float(N - 1), None, ALU.min)
            TS(gat_idx[:, :, 1], dst_f[:, :], float(N - 1), None, ALU.min).then_inc(idx_set, 1)
            ch.step(TS(off_trash[:, :], src_f[:, :], lane[:, :], None, ALU.subtract))
            dve.wait_ge(params_in, 48)
            ch.step(TS(ew2[:, :], ew2[:, :], par[:, 4:5], par[:, 5:6], ALU.mult, ALU.add))
            ch.step(TS(tmp_b[:, :], ew2[:, :], -1.0, None, ALU.mult))
            ch.step(TT(tmp_a[:, :], ew2[:, :], tmp_b[:, :], ALU.min))
            ch.step(V.tensor_reduce(pe_[:, 4:5], par[:, 0:3], AXX, ALU.max))
            ch.step(TS(pe_[:, 0:3], par[:, 0:3], pe_[:, 4:5], None, ALU.subtract))
            ch.step(TS(pe_[:, 5:6], par[:, 3:4], -1.0, None, ALU.mult))
            TT(pe_[:, 3:4], pe_[:, 5:6], par[:, 3:4], ALU.min).then_inc(exp_in, 1)
            dve.wait_ge(exps, 2)
            ch.step(STT(tmp_b[:, :], ew2[:, :], 0.0, tmp_a[:, :], ALU.max, ALU.add))
            ch.step(TT(base[:, :], tmp_b[:, :], ew[:, :], ALU.mult))
            ch.step(TT(tmp_b[:, :], src_f[:, :], dst_f[:, :], ALU.not_equal))
            ch.step(TT(base[:, :], base[:, :], tmp_b[:, :], ALU.mult))
            ch.step(STT(pe_[:, 6:7], par[:, 3:4], 0.0, pe_[:, 3:4], ALU.max, ALU.add))
            ch.step(V.tensor_reduce(pe_[:, 5:6], pe_[:, 0:3], AXX, ALU.add))
            ch.step(V.reciprocal(pe_[:, 7:8], pe_[:, 5:6]))
            ch.step(TS(cs[:, :], pe_[:, 0:3], pe_[:, 7:8], pe_[:, 6:7], ALU.mult, ALU.mult))
            dve.wait_ge(weights_in, 16 * (N_WEIGHT - 3))

            def centre(to, of, mean):
                ch.step(V.tensor_reduce(mean, of, AXX, ALU.add))
                ch.step(TS(mean, mean, 1.0 / F, None, ALU.mult))
                ch.step(TS(to, of, mean, None, ALU.subtract))

            centre(w2c[:, :], w2x[:, :], wmean[:, :])
            centre(brow_c[:, :], brow[:, :], rmean[:, 0:1])
            centre(bn2_c[:, :], bn2_row[:, :], rmean[:, 1:2])
            ch.step(TS(zrow[:, :], brow_c[:, :], cs[:, 2:3], None, ALU.mult))
            for r in range(R):
                V.tensor_copy(zrow8[:, r, :], zrow[0:1, :])
                ch.step(V.tensor_copy(n2row8[:, r, :], bn2_c[0:1, :]))
            ch.step(TT(w2z[:, :], ident[:, 0:F], ident[:, F:P], ALU.add))
            ch.step(TS(w2z[:, :], w2z[:, :], -1.0 / F, None, ALU.add))
            ch.step(STT(w2z[:, :], w2c[:, :], cs[:, 2:3], w2z[:, :], ALU.mult, ALU.add))
            for lo, hi in ((0, F), (F, P)):
                V.tensor_copy(wh_w[lo:hi, lo:hi], w2x[lo:hi, :])
                ch.step(V.tensor_copy(z_w[lo:hi, lo:hi], w2z[lo:hi, :]))
            ch.step(V.tensor_copy(wc_w[F:P, :], w2c[F:P, :]))
            dve.wait_ge(wt_set, 1)
            for lo, hi in ((0, F), (F, P)):
                centre(n2_w[lo:hi, lo:hi], wt[lo:hi, 8, lo:hi], rmean[lo:hi, 2:3])
            V.tensor_copy(rmean[:, 2:3], rmean[:, 1:2]).then_inc(weights_set, 1)
            dve.wait_ge(weights_set, 2)
            dve.wait_ge(ef_in, 32)

            def r8(a):
                return a[:, :].rearrange("p (r f) -> p r f", f=F)

            DENSE_STEPS = 4

            def rsqrt(ch, y, v, w):
                wi = w.bitcast(I32)
                ch.step(TS(wi, v.bitcast(I32), 1, None, ALU.logical_shift_right))
                ch.step(TS(y.bitcast(I32), wi, -1.0, float(0x5F3759DF), ALU.mult, ALU.add))
                for _ in range(3):
                    ch.step(TT(w, y, y, ALU.mult))
                    ch.step(STT(w, w, -0.5, v, ALU.mult, ALU.mult))
                    ch.step(STT(y, w, 1.5, y, ALU.add, ALU.mult))

            def rstd(ch, y, v, w):
                ch.step(TS(v, v, 1.0 / F, EPS_LN, ALU.mult, ALU.add))
                rsqrt(ch, y, v, w)

            def dense_ln1(ch, d):
                wait(dve, sqd_set, d + 1)
                ch.step(V.tensor_reduce(vard[:, :], r8(sqd), AXX, ALU.add))
                rstd(ch, rsd[:, :], vard[:, :], tmpd[:, :])
                TT(r8(x1d), r8(p_e), rsd[:, :].unsqueeze(2).to_broadcast([P, R, F]), ALU.mult).then_inc(x1d_set, 1)

            def dense_v(d):
                wait(dve, od_ps, d + 1)
                wait(dve, x1d_set, d + 1)
                TT(vd[:, :], p_e[:, :], x1d[:, :], ALU.add).then_inc(vd_set, 1)

            def dense_ln2(ch, d):
                wait(dve, sqd2_set, d + 1)
                ch.step(V.tensor_reduce(vard[:, :], r8(sqd), AXX, ALU.add))
                rstd(ch, rsd[:, :], vard[:, :], tmpd[:, :])
                wait(dve, od_out, 16 * d)
                TT(r8(od), r8(vd), rsd[:, :].unsqueeze(2).to_broadcast([P, R, F]), ALU.mult).then_inc(od_set, 1)

            def same_src(i, srcb_in, count, done):
                wait(dve, srcb_in, count)
                TT(same[:, :, :], srcb[:, :, :],
                   src_f[:, bass.ds(i * G, G)].unsqueeze(2).to_broadcast([P, G, P]), ALU.is_equal).then_inc(done, 1)

            def bc(a, n):
                return a.unsqueeze(2).to_broadcast([P, a.shape[1], n])

            A_STEPS = 52
            with dve.Fori(0, GROUPS) as i:
                ch = Chain(dve, a_chain, i * A_STEPS)
                grp = bass.ds(i * G, G)
                wait(dve, a_sum_ps, i)
                same_src(i, a_srcb, 16 * (i + 1), a_same)
                wait(dve, a_same, i + 1)
                ch.step(TT(before[:, :, :], same[:, :, :],
                           lower[:, :].unsqueeze(1).to_broadcast([P, G, P]), ALU.mult))
                ch.step(V.tensor_reduce(cnt[:, :], before[:, :, :], AXX, ALU.add))
                ch.step(TS(cnt[:, :], cnt[:, :], 0.0, None, ALU.is_equal))
                ch.step(TT(cnt[:, :], cnt[:, :], off_trash[:, grp], ALU.mult))
                TS(sct_idx[:, grp], cnt[:, :], lane[:, :], None, ALU.add).then_inc(a_idx, 1)
                dense_ln1(ch, i)
                wait(dve, a_wh_ps, i + 1)
                wait(dve, a_sq, i)
                ch.step(TT(whc[:, :, :], p_b[:, 0:G * F].rearrange("p (g f) -> p g f", f=F),
                           brow_c[:, :].unsqueeze(1).to_broadcast([P, G, F]), ALU.add))
                TT(wh[:, :, :].rearrange("p g (h f) -> p (g h) f", f=F), r8(p_w),
                   brow[:, :].unsqueeze(1).to_broadcast([P, R, F]), ALU.add).then_inc(a_wh, 1)
                TT(y_all[:, grp, :].rearrange("p g (h f) -> p (g h) f", f=F), r8(p_z),
                   zrow[:, :].unsqueeze(1).to_broadcast([P, R, F]), ALU.add).then_inc(a_y, 1)
                wait(dve, a_wh, i + 1)
                ch.step(TT(prod[:, :, :], wh[:, :, 0:F], wh[:, :, F:2 * F], ALU.mult))
                ch.step(V.tensor_reduce(dot[:, :], prod[:, :, :], AXX, ALU.add))
                wait(dve, a_sq, i + 1)
                ch.step(V.tensor_reduce(n2[:, :, :].rearrange("p g h -> p (g h)"),
                                        sq[:, :, :].rearrange("p g (h f) -> p (g h) f", f=F), AXX, ALU.add))
                ch.step(TT(nn[:, :], n2[:, :, 0], n2[:, :, 1], ALU.mult))
                ch.step(TS(nn[:, :], nn[:, :], EPS_SIM ** 2, None, ALU.max))
                rsqrt(ch, rs[:, 0:G], nn[:, :], tmps[:, 0:G])
                ch.step(TT(dot[:, :], dot[:, :], rs[:, 0:G], ALU.mult))
                ch.step(TS(sc1[:, :], dot[:, :], 0.0, cs[:, 0:1], ALU.max, ALU.mult))
                ch.step(TS(sc2[:, :], dot[:, :], 0.0, cs[:, 1:2], ALU.min, ALU.mult))
                ch.step(TT(sc1[:, :], sc1[:, :], sc2[:, :], ALU.add))
                ch.step(TT(sc1[:, :], sc1[:, :], base[:, grp], ALU.mult))
                TT(msg[:, :, :], whc[:, :, :], bc(sc1[:, :], F), ALU.mult).then_inc(a_msg, 1)
                dense_v(i)
                dense_ln2(ch, i)
                assert ch.n == A_STEPS, ch.n

            dve.wait_ge(a_y, GROUPS)
            dve.wait_ge(a_sum_ps, GROUPS)
            B_STEPS = 39
            with dve.Fori(0, GROUPS) as i:
                ch = Chain(dve, b_chain, i * B_STEPS)
                grp = bass.ds(i * G, G)
                for j in range(G):
                    wait(dve, b_pg[j], 32 * (i + 1))
                wait(dve, b_xt_ps, i)
                wait(dve, b_h, i)
                TT(wh[:, :, :], y_all[:, grp, :], xg[:, :, :], ALU.add).then_inc(b_v, 1)
                wait(dve, b_sq, i + 1)
                ch.step(V.tensor_reduce(var[:, :], sq[:, :, :].rearrange("p g (h f) -> p (g h) f", f=F), AXX, ALU.add))
                rstd(ch, rs[:, :], var[:, :], tmps[:, :])
                TT(wh[:, :, :].rearrange("p g (h f) -> p (g h) f", f=F),
                   wh[:, :, :].rearrange("p g (h f) -> p (g h) f", f=F), bc(rs[:, :], F), ALU.mult).then_inc(b_x1, 1)
                wait(dve, b_sum_ps, i)
                same_src(i, b_srcb, 16 * (i + 1), b_same)
                dense_ln1(ch, i + HALF)
                wait(dve, b_m_ps, i + 1)
                wait(dve, b_m, i)
                TT(prod[:, :, :], p_z[:, P:P + G * F].rearrange("p (g f) -> p g f", f=F),
                   be2_row[:, :].unsqueeze(1).to_broadcast([P, G, F]), ALU.add).then_inc(b_m0, 1)
                dense_v(i + HALF)
                dense_ln2(ch, i + HALF)
                assert ch.n == B_STEPS, ch.n

            C_STEPS = 14
            with dve.Fori(0, GROUPS) as i:
                ch = Chain(dve, c_chain, i * C_STEPS)
                wait(dve, c_o_ps, i + 1)
                ch.step(TT(prod[:, :, :], p_z[:, 0:G * F].rearrange("p (g f) -> p g f", f=F),
                           bn2_c[:, :].unsqueeze(1).to_broadcast([P, G, F]), ALU.add))
                TT(wh[:, :, 0:F], prod[:, :, :], xg[:, :, 0:F], ALU.add).then_inc(c_v, 1)
                wait(dve, c_sq, i + 1)
                ch.step(V.tensor_reduce(var[:, 0:G], sq[:, :, 0:F], AXX, ALU.add))
                rstd(ch, rs[:, 0:G], var[:, 0:G], tmps[:, 0:G])
                wait(dve, c_sct, 16 * G * i)
                TT(sm[:, :, :], wh[:, :, 0:F], bc(rs[:, 0:G], F), ALU.mult).then_inc(c_out, 1)
                assert ch.n == C_STEPS, ch.n


_INS = ['x', 'src', 'dst', 'edge_attr_32', 'edge_weight', 'edge_weight_n2', 'L0_gnn_W', 'L0_gnn_b',
        'L0_gnn_deg_coeff', 'L0_gnn_coeff_param', 'L0_gnn_scale_param', 'L1_gnn_We1', 'L1_gnn_be1', 'L1_gnn_We2',
        'L1_gnn_be2', 'L1_gnn_Wn1', 'L1_gnn_bn1', 'L1_gnn_Wn2', 'L1_gnn_bn2']
_OUTS = [((100000, 64), 'float32')]


def kernel(**inputs):
    import numpy as _np
    import concourse.bacc as _bacc
    from concourse import mybir as _mybir
    from concourse.bass_utils import run_bass_kernel_spmd as _run

    nc = _bacc.Bacc("TRN2", target_bir_lowering=False, num_devices=1)
    arrays, args = {}, []
    for name in _INS:
        a = _np.ascontiguousarray(inputs[name])
        arrays[f"in_{name}_dram"] = a
        args.append(nc.dram_tensor(f"in_{name}_dram", a.shape, _mybir.dt.from_np(a.dtype), kind="ExternalInput").ap())
    for i, (shape, dtype) in enumerate(_OUTS):
        dt = _mybir.dt.from_np(_np.dtype(dtype))
        args.append(nc.dram_tensor(f"out_{i}_dram", shape, dt, kind="ExternalOutput").ap())
    gnn(nc, *args)
    r = _run(nc, [arrays], core_ids=[0])
    return r.results[0]["out_0_dram"]
```

```python
import concourse.bass as bass
from concourse import mybir
from contextlib import ExitStack

F32 = mybir.dt.float32
I32 = mybir.dt.int32
ALU = mybir.AluOpType
ACT = mybir.ActivationFunctionType
AXX = mybir.AxisListType.X


class Chain:

    def __init__(self, eng, sem):
        self.eng, self.sem, self.n, self.passed = eng, sem, 0, 0

    def mark(self, ins):
        ins.then_inc(self.sem, 1)
        self.n += 1
        return self.n

    def need(self, n):
        self.eng.wait_ge(self.sem, self.passed + n)
        self.eng.nop(nofuse=True)

    def step(self, ins):
        self.need(self.mark(ins))


def wait(eng, sem, value):
    if isinstance(value, int) and value <= 0:
        return
    eng.wait_ge(sem, value)
    eng.nop(nofuse=True)


LAG = 5


def over_groups(eng, groups, body, chain=None, per_pass=0):
    pairs = (groups - LAG) // 2
    assert LAG + 2 * pairs == groups
    for i in range(LAG):
        body(i, i % 2, i // 2)
    n = chain.n if chain else 0
    with eng.Fori(0, pairs) as k:
        if chain:
            chain.passed = k * per_pass
        body(k * 2 + LAG, LAG % 2, k + LAG // 2)
        body(k * 2 + LAG + 1, (LAG + 1) % 2, k + (LAG + 1) // 2)
    if chain:
        assert chain.n - n == per_pass, chain.n - n
        chain.n, chain.passed = n + pairs * per_pass, 0
    for i in range(groups, groups + LAG):
        body(i, i % 2, i // 2)


def gnn(nc, x, src, dst, edge_attr, edge_w, edge_w2, W, b, deg_coeff, coeff_param, scale_param,
        We1, be1, We2, be2, Wn1, bn1, Wn2, bn2, out):
    N, F = x.shape
    E, EF = edge_attr.shape
    P = 128
    T = -(-E // P)
    G = 4
    GROUPS = T // G
    assert T == GROUPS * G
    FULL = E // T
    REST = E - FULL * T
    assert FULL == P - 1
    TRASH = N
    R = 8
    CH = P * R
    HALF = GROUPS
    B_STEP = -(-(N - CH - HALF * CH) // (HALF - 1))
    B0 = N - CH - (HALF - 1) * B_STEP
    assert B0 <= HALF * CH and B_STEP <= CH
    EPS_LN, EPS_SIM = 1e-5, 1e-8

    ZR = -(-(N + P) // (GROUPS * P)) * P
    sums = nc.dram_tensor("prop_sums", [GROUPS * ZR, F], F32, kind="Internal").ap()
    aggs = nc.dram_tensor("message_sums", [GROUPS * ZR, F], F32, kind="Internal").ap()
    src_rows = nc.dram_tensor("src_rows", [1 + T, P], F32, kind="Internal").ap()

    ctx = ExitStack()
    with ctx:
        def sb(name, shape, dt=F32):
            return ctx.enter_context(nc.sbuf_tensor(name, shape, dt))

        def ps(name):
            return ctx.enter_context(nc.psum_tensor(name, [P, 512], F32))

        def sem(name):
            return ctx.enter_context(nc.semaphore(name))

        ident = sb("ident", [P, P])
        lower = sb("lower", [P, P])
        ones = sb("ones", [1, P])
        no_src = sb("no_src", [1, P])
        lane = sb("lane", [P, 1])
        wt = sb("wt", [P, 9, P])
        w2x = sb("w2x", [P, F])
        wmean = sb("wmean", [P, 1])
        w2c = sb("w2c", [P, F])
        w2z = sb("w2z", [P, F])
        wh_w = sb("wh_w", [P, P])
        wc_w = sb("wc_w", [P, F])
        z_w = sb("z_w", [P, P])
        n2_w = sb("n2_w", [P, P])
        brow = sb("brow", [P, F])
        brow_c = sb("brow_c", [P, F])
        zrow = sb("zrow", [P, F])
        be2_row = sb("be2_row", [P, F])
        bn2_row = sb("bn2_row", [P, F])
        bn2_c = sb("bn2_c", [P, F])
        zrow8 = sb("zrow8", [1, R, F])
        n2row8 = sb("n2row8", [1, R, F])
        rmean = sb("rmean", [P, 3])
        be1_col = sb("be1_col", [F, 1])
        bn1_col = sb("bn1_col", [P, 1])
        par = sb("par", [P, 6])
        pe_ = sb("par_e", [P, 8])
        cs = sb("cs", [P, 3])
        src_i = sb("src_i", [P, T], I32)
        dst_i = sb("dst_i", [P, T], I32)
        src_f = sb("src_f", [P, T])
        dst_f = sb("dst_f", [P, T])
        base = sb("base", [P, T])
        ew = sb("ew", [P, T])
        ew2 = sb("ew2", [P, T])
        tmp_a = sb("tmp_a", [P, T])
        tmp_b = sb("tmp_b", [P, T])
        gat_idx = sb("gat_idx", [P, T + 2 * G, 2], I32)
        off_trash = sb("off_trash", [P, T])
        sct_idx = sb("sct_idx", [P, T], I32)
        ef = sb("ef", [P, T, EF])
        srct = sb("srct", [P, 2, P])
        y_all = sb("y_all", [P, T, 2 * F])
        stage = y_all[:, 0:9, :]
        gi = [sb(f"gi{q}", [P, G, 2], I32) for q in range(2)]
        si = [sb(f"si{q}", [P, G], I32) for q in range(2)]
        xg = [sb(f"xg{q}", [P, G, 2 * F]) for q in range(2)]
        xt = sb("xt", [P, G * P])
        efg = sb("efg", [P, P])
        eft = sb("eft", [P, P])
        ht = sb("ht", [F, G * P])
        srcb = sb("srcb", [P, G, P])
        same = [sb(f"same{q}", [P, G, P]) for q in range(2)]
        before = sb("before", [P, G, P])
        wh = sb("wh", [P, G, 2 * F])
        whc = [sb(f"whc{q}", [P, G, F]) for q in range(2)]
        sq = sb("sq", [P, G, 2 * F])
        prod = sb("prod", [P, G, F])
        n2 = sb("n2", [P, G, 2])
        nn = sb("nn", [P, G])
        dot = [sb(f"dot{q}", [P, G]) for q in range(2)]
        sc1 = sb("sc1", [P, G])
        sc2 = sb("sc2", [P, G])
        cnt = sb("cnt", [P, G])
        msg = sb("msg", [P, G, F])
        x1e = sb("x1e", [P, G, 2 * F])
        sm = [sb(f"sm{q}", [P, G, F]) for q in range(2)]
        NE = 2 * G
        raw = sb("raw", [P, NE + 2 * R])
        rv = sb("rv", [P, NE + 2 * R])
        ry = sb("ry", [P, NE + 2 * R])
        rw = sb("rw", [P, NE + 2 * R])
        xd = sb("xd", [P, R * F])
        xdt = sb("xdt", [P, R * F])
        x1t = sb("x1t", [P, R * F])
        sqd = sb("sqd", [P, R * F])
        sqv = sb("sqv", [P, R * F])
        x1d = [sb(f"x1d{q}", [P, R * F]) for q in range(2)]
        hd = sb("hd", [P, R * F])
        vd = sb("vd", [P, R * F])
        od = sb("od", [P, R * F])
        zero = sb("zero", [P, ZR // P * F])

        p_t, p_x, p_w, p_z, p_s, p_d, p_e, p_o = (ps(n) for n in
                                                  ("p_t", "p_x", "p_w", "p_z", "p_s", "p_d", "p_e", "p_o"))

        pads_set = sem("pads_set"); zero_set = sem("zero_set"); consts_set = sem("consts_set")
        edges_in = sem("edges_in"); weights_in = sem("weights_in"); params_in = sem("params_in")
        sums_zero = sem("sums_zero"); aggs_zero = sem("aggs_zero"); ef_in = sem("ef_in")
        wt_ps = sem("wt_ps"); wt_set = sem("wt_set"); weights_set = sem("weights_set")
        srct_ps = sem("srct_ps"); srct_set = sem("srct_set"); src_rows_out = sem("src_rows_out")
        exps = sem("exps"); exp_in = sem("exp_in"); idx_set = sem("idx_set"); src_f_set = sem("src_f_set")
        dve_chain = sem("dve_chain"); pool_chain = sem("pool_chain")
        xd_in = sem("xd_in"); xd_t = sem("xd_t"); xdt_set = sem("xdt_set"); zd_ps = sem("zd_ps")
        sqd_set = sem("sqd_set"); var1_set = sem("var1_set"); x1d_set = sem("x1d_set"); x1d_t = sem("x1d_t")
        x1t_set = sem("x1t_set"); hd_ps = sem("hd_ps"); hd_set = sem("hd_set"); od_ps = sem("od_ps")
        vd_set = sem("vd_set"); sqv_set = sem("sqv_set"); var2_set = sem("var2_set")
        od_set = sem("od_set"); od_out = sem("od_out")
        a_gi = sem("a_gi"); a_xg = [sem("a_xg0"), sem("a_xg1")]
        a_srcb = sem("a_srcb"); a_same = sem("a_same"); a_idx = sem("a_idx")
        a_xt_ps = sem("a_xt_ps"); a_xt = sem("a_xt"); a_wh_ps = sem("a_wh_ps"); a_wh = sem("a_wh"); a_y = sem("a_y")
        a_sq = sem("a_sq"); a_n2 = sem("a_n2"); a_msg = sem("a_msg"); a_sum_ps = sem("a_sum_ps")
        a_sum = sem("a_sum"); a_acc = sem("a_acc"); a_chain = sem("a_chain")
        b_gi = sem("b_gi"); b_pg = [sem("b_pg0"), sem("b_pg1")]
        b_srcb = sem("b_srcb"); b_same = sem("b_same"); b_v = sem("b_v"); b_sq = sem("b_sq"); b_var = sem("b_var")
        b_x1 = sem("b_x1"); b_ef = sem("b_ef"); b_xt_ps = sem("b_xt_ps"); b_xt = sem("b_xt"); b_keep = sem("b_keep")
        b_h_ps = sem("b_h_ps"); b_h = sem("b_h"); b_m_ps = sem("b_m_ps"); b_m0 = sem("b_m0"); b_m = sem("b_m")
        b_sum_ps = sem("b_sum_ps"); b_sum = sem("b_sum"); b_acc = sem("b_acc"); b_chain = sem("b_chain")
        c_gi = sem("c_gi"); c_ag = [sem("c_ag0"), sem("c_ag1")]
        c_srcb = sem("c_srcb"); c_idx = sem("c_idx"); c_eq = sem("c_eq"); c_x1 = sem("c_x1"); c_xt_ps = sem("c_xt_ps")
        c_xt = sem("c_xt"); c_h_ps = sem("c_h_ps"); c_h = sem("c_h"); c_o_ps = sem("c_o_ps"); c_v = sem("c_v")
        c_sq = sem("c_sq"); c_var = sem("c_var"); c_out = sem("c_out"); c_sct = [sem("c_sct0"), sem("c_sct1")]
        c_chain = sem("c_chain")

        def min_int(a, b):
            return min(a, b) if isinstance(a, int) else a

        def live(i):
            return not isinstance(i, int) or 0 <= i < GROUPS

        def grp(i):
            return bass.ds(i * G, G)

        def per_edge(a):
            return a[0:FULL * T].rearrange("(p t) -> p t", t=T), a[FULL * T:E].rearrange("(a t) -> a t", a=1)

        def row(a, n=P):
            return a.rearrange("(a f) -> a f", a=1).to_broadcast([n, a.shape[0]])

        N_EDGE = 8
        N_WEIGHT = 22
        block = ctx.enter_context(nc.Block())

        @block.sync
        def _(sp):
            sp.wait_ge(pads_set, 1)
            for a, t in ((src, src_i), (dst, dst_i), (edge_w, ew), (edge_w2, ew2)):
                whole, rest = per_edge(a)
                sp.dma_start(t[0:FULL, :], whole).then_inc(edges_in, 16)
                sp.dma_start(t[FULL:P, 0:REST], rest).then_inc(edges_in, 16)
            sp.dma_start(par[:, 0:3], row(coeff_param)).then_inc(params_in, 16)
            sp.dma_start(par[:, 3:4], row(scale_param)).then_inc(params_in, 16)
            sp.dma_start(par[:, 4:6], row(deg_coeff)).then_inc(params_in, 16)
            loads = [(w2x[0:F, :], W), (w2x[F:P, :], W), (stage[0:F, 0, :], We1[:, 0:P])]
            loads += [(stage[0:F, 1 + j, EF * j:EF * (j + 1)], We1[:, P:P + EF]) for j in range(G)]
            loads += [(stage[0:F, 5, 0:F], We2), (stage[0:F, 6, :], Wn1),
                      (stage[0:F, 7, 0:F], Wn1[:, 0:F]), (stage[F:P, 7, F:P], Wn1[:, 0:F]),
                      (stage[0:F, 8, 0:F], Wn2), (stage[F:P, 8, F:P], Wn2),
                      (brow[:, :], row(b)), (be2_row[:, :], row(be2)), (bn2_row[:, :], row(bn2)),
                      (be1_col[:, :], be1.rearrange("(f a) -> f a", a=1)),
                      (bn1_col[0:F, :], bn1.rearrange("(f a) -> f a", a=1)),
                      (bn1_col[F:P, :], bn1.rearrange("(f a) -> f a", a=1))]
            sp.wait_ge(zero_set, 2)
            for to, of in loads:
                sp.dma_start(to, of).then_inc(weights_in, 16)
            assert len(loads) == N_WEIGHT - 3
            sp.dma_start(sums.rearrange("(c p r) f -> p c (r f)", p=P, c=GROUPS),
                         zero[:, :].unsqueeze(1).to_broadcast([P, GROUPS, ZR // P * F])).then_inc(sums_zero, 16)
            sp.dma_start(ef[0:FULL, :, :], edge_attr[0:FULL * T, :].rearrange("(p t) f -> p t f", t=T)).then_inc(ef_in, 16)
            sp.dma_start(ef[FULL:P, 0:REST, :], edge_attr[FULL * T:E, :].rearrange("(a t) f -> a t f", a=1)).then_inc(ef_in, 16)
            sp.wait_ge(srct_set, 1)
            sp.dma_start(src_rows[0:1, :], no_src[:, :]).then_inc(src_rows_out, 16)
            sp.dma_start(src_rows[1:1 + P, :], srct[:, 0, :]).then_inc(src_rows_out, 16)
            sp.dma_start(src_rows[1 + P:1 + T, :], srct[0:T - P, 1, :]).then_inc(src_rows_out, 16)
            sp.wait_ge(src_rows_out, 48)

            def chunk(a, r0):
                return a[bass.ds(r0, CH), :].rearrange("(p r) f -> p (r f)", r=R)

            def load_srcb(row0, sem_in):
                sp.dma_start(srcb[:, :, :].rearrange("p g e -> p (g e)"),
                             src_rows[bass.ds(row0, G), :].rearrange("(a g) e -> a (g e)", a=1)
                             .to_broadcast([P, G * P])).then_inc(sem_in, 16)

            def dense_io(i, d0, row_of):
                if live(i):
                    wait(sp, xd_t, i + d0)
                    sp.dma_start(xd[:, :], chunk(x, row_of(i))).then_inc(xd_in, 16)
                if live(i - 5):
                    wait(sp, od_set, i - 5 + d0 + 1)
                    wait(sp, od_out, (i - 5 + d0) * 16)
                    sp.dma_start(chunk(out, row_of(i - 5)), od[:, :]).then_inc(od_out, 16)

            def body_a(i, q, h):
                if live(i - 1):
                    wait(sp, a_same, i - 1)
                    load_srcb((i - 1) * G + 1, a_srcb)
                dense_io(i, 0, lambda n: n * CH)
                if live(i):
                    sp.dma_start(aggs[bass.ds(i * ZR, ZR), :].rearrange("(p r) f -> p (r f)", p=P), zero[:, :])\
                      .then_inc(aggs_zero, 16)

            def body_b(i, q, h):
                if live(i - 2):
                    wait(sp, b_same, i - 2)
                    load_srcb((i - 2) * G + 1, b_srcb)
                dense_io(i, HALF, lambda n: n * B_STEP + B0)

            def body_c(i, q, h):
                if live(i):
                    wait(sp, c_eq, i)
                    load_srcb(i * G, c_srcb)

            over_groups(sp, GROUPS, body_a)
            sp.wait_ge(a_same, GROUPS)
            over_groups(sp, GROUPS, body_b)
            sp.wait_ge(b_same, GROUPS)
            over_groups(sp, GROUPS, body_c)
            sp.wait_ge(od_out, 16 * 2 * HALF)

        @block.gpsimd
        def _(pool):
            ch = Chain(pool, pool_chain)
            ch.step(nc.gpsimd.memset(ident[:, :], 0.0))
            ch.step(nc.gpsimd.affine_select(out=ident[:, :], in_=ident[:, :], compare_op=ALU.not_equal, fill=1.0,
                                            base=0, pattern=[[-1, P]], channel_multiplier=1))
            ch.step(nc.gpsimd.memset(lower[:, :], 1.0))
            ch.step(nc.gpsimd.affine_select(out=lower[:, :], in_=lower[:, :], compare_op=ALU.is_gt, fill=0.0,
                                            base=0, pattern=[[-1, P]], channel_multiplier=1))
            ch.step(nc.gpsimd.iota(lane[:, :], pattern=[[0, 1]], base=N, channel_multiplier=1,
                                   allow_small_or_imprecise_dtypes=True))
            ch.step(nc.gpsimd.memset(no_src[:, :], -1.0))
            nc.gpsimd.memset(ones[:, :], 1.0).then_inc(consts_set, 1)

            def gather(to, table, index, done):
                nc.gpsimd.indirect_dma_start(to, None, table, bass.IndirectOffsetOnAxis(ap=index, axis=0))\
                    .then_inc(done, 16)

            def add(table, q, j, tile, acc):
                wait(pool, acc, tile * 16)
                nc.gpsimd.indirect_dma_start(table, bass.IndirectOffsetOnAxis(ap=si[q][:, j:j + 1], axis=0),
                                             sm[q][:, j, :], None, compute_op=ALU.add).then_inc(acc, 16)

            def gather_both(table, q, j, done):
                gather(xg[q][:, j, 0:F], table, gi[q][:, j, 0:1], done[q])
                gather(xg[q][:, j, F:2 * F], table, gi[q][:, j, 1:2], done[q])

            def body_a(i, q, h):
                if live(i):
                    wait(pool, a_gi, i + 1)
                    wait(pool, a_xt_ps, i - 1)
                if live(i - 5):
                    wait(pool, a_sum, i - 5 + 1)
                for j in range(G):
                    if live(i):
                        gather_both(x, q, j, a_xg)
                    if live(i - 5):
                        add(sums, 1 - q, j, (i - 5) * G + j, a_acc)
                if isinstance(i, int) and i == 4:
                    pool.wait_ge(sums_zero, 16)

            over_groups(pool, GROUPS, body_a)
            pool.wait_ge(a_acc, 16 * T)

            def body_b(i, q, h):
                if live(i):
                    wait(pool, b_gi, i + 1)
                    wait(pool, b_v, i - 1)
                if live(i - 5):
                    wait(pool, b_sum, i - 5 + 1)
                for j in range(G):
                    if live(i):
                        gather_both(sums, q, j, b_pg)
                    if live(i - 5):
                        add(aggs, 1 - q, j, (i - 5) * G + j, b_acc)
                if isinstance(i, int) and i == 4:
                    pool.wait_ge(aggs_zero, 16 * GROUPS)

            over_groups(pool, GROUPS, body_b)
            pool.wait_ge(b_acc, 16 * T)

            def body_c(i, q, h):
                if live(i):
                    wait(pool, c_gi, i + 1)
                    wait(pool, c_xt_ps, i - 1)
                if live(i - 3):
                    wait(pool, c_out, i - 3 + 1)
                    wait(pool, c_idx, i - 3 + 1)
                for j in range(G):
                    if live(i):
                        gather(xg[q][:, j, F:2 * F], aggs, gi[q][:, j, 0:1], c_ag[q])
                    if live(i - 3):
                        wait(pool, c_sct[j % 2], ((i - 3) * (G // 2) + j // 2) * 16)
                        nc.gpsimd.indirect_dma_start(out, bass.IndirectOffsetOnAxis(ap=si[1 - q][:, j:j + 1], axis=0),
                                                     sm[1 - q][:, j, :], None, bounds_check=N - 1, oob_is_err=False)\
                            .then_inc(c_sct[j % 2], 16)
                if isinstance(i, int) and i == 2:
                    pool.wait_ge(od_out, 16 * 2 * HALF)

            over_groups(pool, GROUPS, body_c)
            for done in c_sct:
                pool.wait_ge(done, 16 * T // 2)

        @block.tensor
        def _(pe):
            mm, tr = nc.tensor.matmul, nc.tensor.transpose

            pe.wait_ge(consts_set, 1)
            pe.wait_ge(src_f_set, 1)
            tr(p_t[:, 0:P], src_f[:, 0:P], ident[:, :])
            tr(p_t[0:T - P, P:2 * P], src_f[:, P:T], ident[:, :]).then_inc(srct_ps, 1)
            pe.wait_ge(weights_in, 16 * (N_WEIGHT - 3))
            for k in range(9):
                last = tr((p_w, p_z, p_s)[k // 4][:, (k % 4) * P:(k % 4 + 1) * P], stage[:, k, :], ident[:, :])
            last.then_inc(wt_ps, 1)
            pe.wait_ge(weights_set, 2)

            def dense_in(d):
                wait(pe, xd_in, d * 16 + 16)
                wait(pe, xdt_set, d)
                for k in range(4):
                    last = tr(p_d[:, k * P:(k + 1) * P], xd[:, k * P:(k + 1) * P], ident[:, :])
                last.then_inc(xd_t, 1)

            def with_row(p, left, right, biases):
                for k in range(4):
                    s = slice(k * P, (k + 1) * P)
                    mm(p[:, s], left[:, s], right, start=True, stop=False)
                    last = mm(p[:, s], ones[:, :], biases[:, 2 * k:2 * k + 2, :].rearrange("a r f -> a (r f)"),
                              start=False, stop=True)
                return last

            def dense_z(d):
                wait(pe, xdt_set, d + 1)
                wait(pe, x1d_set, d)
                with_row(p_e, xdt, z_w[:, :], zrow8).then_inc(zd_ps, 1)

            def dense_t(d, q):
                wait(pe, x1d_set, d + 1)
                wait(pe, x1t_set, d)
                for k in range(4):
                    last = tr(p_x[:, k * P:(k + 1) * P], x1d[q][:, k * P:(k + 1) * P], ident[:, :])
                last.then_inc(x1d_t, 1)

            def dense_h(d):
                wait(pe, x1t_set, d + 1)
                mm(p_t[:, :], wt[:, 7, :], x1t[:, :], start=True, stop=True).then_inc(hd_ps, 1)

            def dense_o(d):
                wait(pe, hd_set, d + 1)
                wait(pe, vd_set, d)
                with_row(p_o, hd, n2_w[:, :], n2row8).then_inc(od_ps, 1)

            def group_sum(p, q, done):
                for j in range(G):
                    last = mm(p[:, j * F:(j + 1) * F], same[q][:, j, :], msg[:, j, :], start=True, stop=True)
                last.then_inc(done, 1)

            def body_a(i, q, h):
                d = i - 3
                if live(i):
                    wait(pe, a_xt, i)
                    wait(pe, hd_set, i - 3)
                    wait(pe, a_xg[q], (h + 1) * (32 * G))
                    for j in range(G):
                        last = tr(p_t[:, j * P:(j + 1) * P], xg[q][:, j, :], ident[:, :])
                    last.then_inc(a_xt_ps, 1)
                if live(d):
                    wait(pe, a_sum, i - 3)
                    dense_t(d, 1 - q)
                if live(i):
                    dense_in(i)
                if live(d):
                    wait(pe, a_xt, min_int(i + 1, GROUPS))
                    dense_h(d)
                    wait(pe, a_msg, i - 3 + 1)
                    wait(pe, a_same, i - 3 + 1)
                    group_sum(p_x, 1 - q, a_sum_ps)
                if live(i):
                    wait(pe, a_xt, i + 1)
                    wait(pe, a_wh, i)
                    wait(pe, a_y, i)
                    for j in range(G):
                        lhs = xt[:, j * P:(j + 1) * P]
                        mm(p_w[:, j * P:(j + 1) * P], lhs, wh_w[:, :], start=True, stop=True)
                        mm(p_z[:, j * P:(j + 1) * P], lhs, z_w[:, :], start=True, stop=True)
                        last = mm(p_s[:, j * F:(j + 1) * F], lhs, wc_w[:, :], start=True, stop=True)
                    last.then_inc(a_wh_ps, 1)
                if live(i - 1):
                    dense_z(i - 1)
                if live(d):
                    dense_o(d)

            def body_b(i, q, h):
                g, d = i - 2, i - 3 + HALF
                if live(g):
                    wait(pe, b_x1, g + 1)
                    wait(pe, hd_set, d)
                    for j in range(G):
                        tr(p_t[:, j * P:(j + 1) * P], x1e[:, j, :], ident[:, :])
                    wait(pe, b_ef, g + 1)
                    wait(pe, x1t_set, min_int(d, 2 * HALF))
                    tr(p_x[:, 0:P], efg[:, :], ident[:, :]).then_inc(b_xt_ps, 1)
                if live(i):
                    dense_in(i + HALF)
                if live(i - 3):
                    wait(pe, b_xt, min_int(g + 1, GROUPS))
                    dense_t(d, 1 - q)
                if live(g):
                    wait(pe, b_xt, g + 1)
                    wait(pe, b_h, g)
                    for j in range(G):
                        s = slice(j * P, (j + 1) * P)
                        mm(p_w[0:F, s], wt[:, 0, 0:F], xt[:, s], start=True, stop=False)
                        last = mm(p_w[0:F, s], wt[:, 1 + j, 0:F], eft[:, :], start=False, stop=True)
                    last.then_inc(b_h_ps, 1)
                if live(i - 3):
                    dense_h(d)
                if live(i - 1):
                    dense_z(i - 1 + HALF)
                if live(g):
                    wait(pe, b_h, g + 1)
                    wait(pe, b_m0, g)
                    for j in range(G):
                        last = mm(p_z[:, j * F:(j + 1) * F], ht[:, j * P:(j + 1) * P], wt[0:F, 5, 0:F],
                                  start=True, stop=True)
                    last.then_inc(b_m_ps, 1)
                if live(i - 3):
                    dense_o(d)
                    wait(pe, b_m, i - 3 + 1)
                    wait(pe, b_same, i - 3 + 1)
                    wait(pe, b_sum, i - 3)
                    group_sum(p_s, 1 - q, b_sum_ps)

            def body_c(i, q, h):
                if live(i):
                    wait(pe, c_ag[q], (h + 1) * (16 * G))
                    wait(pe, c_x1, i + 1)
                    wait(pe, c_xt, i)
                    for j in range(G):
                        last = tr(p_t[:, j * P:(j + 1) * P], xg[q][:, j, :], ident[:, :])
                    last.then_inc(c_xt_ps, 1)
                    wait(pe, c_xt, i + 1)
                    wait(pe, c_h, i)
                    mm(p_w[0:F, :], wt[:, 6, 0:F], xt[:, :], start=True, stop=True).then_inc(c_h_ps, 1)
                    wait(pe, c_h, i + 1)
                    wait(pe, c_v, i)
                    for j in range(G):
                        last = mm(p_z[:, j * F:(j + 1) * F], ht[:, j * P:(j + 1) * P], n2_w[0:F, 0:F],
                                  start=True, stop=True)
                    last.then_inc(c_o_ps, 1)

            over_groups(pe, GROUPS, body_a)
            over_groups(pe, GROUPS, body_b)
            over_groups(pe, GROUPS, body_c)

        @block.scalar
        def _(act):
            A = nc.scalar.activation
            act.wait_ge(exp_in, 1)
            A(pe_[:, 0:4], pe_[:, 0:4], ACT.Exp)
            A(tmp_a[:, :], tmp_a[:, :], ACT.Exp).then_inc(exps, 1)
            act.wait_ge(exps, 1)
            A(pe_[:, 3:4], pe_[:, 3:4], ACT.Ln, bias=1.0)
            A(tmp_a[:, :], tmp_a[:, :], ACT.Ln, bias=1.0).then_inc(exps, 1)
            act.wait_ge(srct_ps, 1)
            nc.scalar.copy(srct[:, 0, :], p_t[:, 0:P])
            nc.scalar.copy(srct[0:T - P, 1, :], p_t[0:T - P, P:2 * P]).then_inc(srct_set, 1)
            act.wait_ge(wt_ps, 1)
            nc.scalar.copy(wt[:, 0:4, :].rearrange("p k f -> p (k f)"), p_w[:, :])
            nc.scalar.copy(wt[:, 4:8, :].rearrange("p k f -> p (k f)"), p_z[:, :])
            nc.scalar.copy(wt[:, 8, :], p_s[:, 0:P]).then_inc(wt_set, 1)
            act.wait_ge(wt_set, 1)
            nc.scalar.copy(ht[0:1, 0:1], be1_col[0:1, :]).then_inc(weights_set, 1)

            A(xt[0:1, 0:1], be1_col[0:1, :], ACT.Silu)

            def copy_gi(i, q, done):
                nc.scalar.copy(gi[q][:, :, :], gat_idx[:, grp(i), :]).then_inc(done, 1)

            def dense_xt(d):
                wait(act, xd_t, d + 1)
                wait(act, zd_ps, d)
                nc.scalar.copy(xdt[:, :], p_d[:, :]).then_inc(xdt_set, 1)

            def dense_sq(d):
                wait(act, zd_ps, d + 1)
                wait(act, var1_set, d)
                A(sqd[:, :], p_e[:, :], ACT.Square).then_inc(sqd_set, 1)

            def dense_x1t(d):
                wait(act, x1d_t, d + 1)
                wait(act, hd_ps, d)
                nc.scalar.copy(x1t[:, :], p_x[:, :]).then_inc(x1t_set, 1)

            def dense_silu(d):
                wait(act, hd_ps, d + 1)
                wait(act, od_ps, d)
                A(hd[:, :], p_t[:, :], ACT.Silu, bias=bn1_col[:, :]).then_inc(hd_set, 1)

            def dense_sqv(d):
                wait(act, vd_set, d + 1)
                wait(act, var2_set, d)
                A(sqv[:, :], vd[:, :], ACT.Square).then_inc(sqv_set, 1)

            def keep_sum(p, g, q, sum_ps, acc, done):
                wait(act, sum_ps, g + 1)
                wait(act, acc, (g - 1) * (16 * G))
                nc.scalar.copy(si[q][:, :], sct_idx[:, grp(g)])
                nc.scalar.copy(sm[q][:, :, :].rearrange("p g f -> p (g f)"), p[:, 0:G * F]).then_inc(done, 1)

            def body_a(i, q, h):
                if live(i):
                    wait(act, a_xt_ps, i + 1)
                    wait(act, a_wh_ps, i)
                    nc.scalar.copy(xt[:, :], p_t[:, :]).then_inc(a_xt, 1)
                    copy_gi(i + 2, q, a_gi)
                if live(i - 3):
                    dense_x1t(i - 3)
                if live(i - 1):
                    wait(act, a_wh, i)
                    wait(act, a_n2, i - 1)
                    A(sq[:, :, :], wh[:, :, :], ACT.Square).then_inc(a_sq, 1)
                if live(i - 3):
                    dense_silu(i - 3)
                    wait(act, a_idx, i - 3 + 1)
                    keep_sum(p_x, i - 3, 1 - q, a_sum_ps, a_acc, a_sum)
                if live(i - 4):
                    dense_sqv(i - 4)
                if live(i - 1):
                    dense_sq(i - 1)
                if live(i):
                    dense_xt(i)

            def body_b(i, q, h):
                g = i - 2
                if live(i - 1):
                    wait(act, b_xt_ps, i - 1)
                    nc.scalar.copy(efg[:, :], ef[:, grp(i - 1), :].rearrange("p g f -> p (g f)")).then_inc(b_ef, 1)
                if live(g):
                    wait(act, b_xt_ps, g + 1)
                    wait(act, b_h_ps, g)
                    nc.scalar.copy(xt[:, :], p_t[:, :])
                    nc.scalar.copy(eft[:, :], p_x[:, 0:P]).then_inc(b_xt, 1)
                    nc.scalar.copy(y_all[:, grp(g), 0:F], x1e[:, :, 0:F]).then_inc(b_keep, 1)
                if live(i - 3):
                    dense_x1t(i - 3 + HALF)
                    wait(act, b_m0, i - 3 + 1)
                    wait(act, b_sum_ps, i - 3)
                    A(msg[:, :, :], prod[:, :, :], ACT.Silu).then_inc(b_m, 1)
                if live(g):
                    wait(act, b_h_ps, g + 1)
                    wait(act, b_m_ps, g)
                    A(ht[:, :], p_w[0:F, :], ACT.Silu, bias=be1_col[:, :]).then_inc(b_h, 1)
                if live(i - 3):
                    dense_silu(i - 3 + HALF)
                if live(i - 4):
                    dense_sqv(i - 4 + HALF)
                if live(i):
                    wait(act, b_v, i + 1)
                    wait(act, b_var, i)
                    A(sq[:, :, :], wh[:, :, :], ACT.Square).then_inc(b_sq, 1)
                    copy_gi(i + 2, q, b_gi)
                if live(i - 1):
                    dense_sq(i - 1 + HALF)
                if live(i):
                    dense_xt(i + HALF)
                if live(i - 3):
                    keep_sum(p_s, i - 3, 1 - q, b_sum_ps, b_acc, b_sum)

            def body_c(i, q, h):
                if live(i):
                    wait(act, c_xt_ps, i - 1)
                    nc.scalar.copy(xg[q][:, :, 0:F], y_all[:, grp(i), 0:F]).then_inc(c_x1, 1)
                if live(i - 1):
                    wait(act, c_v, i)
                    wait(act, c_var, i - 1)
                    A(sq[:, :, 0:F], wh[:, :, 0:F], ACT.Square).then_inc(c_sq, 1)
                if live(i):
                    wait(act, c_xt_ps, i + 1)
                    wait(act, c_h_ps, i)
                    nc.scalar.copy(xt[:, :], p_t[:, :]).then_inc(c_xt, 1)
                    wait(act, c_h_ps, i + 1)
                    wait(act, c_o_ps, i)
                    A(ht[:, :], p_w[0:F, :], ACT.Silu, bias=bn1_col[0:F, :]).then_inc(c_h, 1)
                    copy_gi(i + 2, q, c_gi)

            def first_gi(done):
                copy_gi(0, 0, done)
                copy_gi(1, 1, done)

            act.wait_ge(idx_set, 1)
            first_gi(a_gi)
            over_groups(act, GROUPS, body_a)
            act.wait_ge(a_acc, 16 * T)
            first_gi(b_gi)
            over_groups(act, GROUPS, body_b)
            act.wait_ge(b_acc, 16 * T)
            first_gi(c_gi)
            over_groups(act, GROUPS, body_c)

        @block.vector
        def _(dve):
            V = nc.vector
            TT, TS, STT = V.tensor_tensor, V.tensor_scalar, V.scalar_tensor_tensor
            V.memset(src_i[96:P, :], N + P - 1)
            V.memset(dst_i[96:P, :], 0)
            V.memset(ew[96:P, :], 0.0)
            V.memset(ew2[96:P, :], 0.0).then_inc(pads_set, 1)
            V.memset(ef[96:P, :, :], 0.0).then_inc(zero_set, 1)
            V.memset(zero[:, :], 0.0)
            V.memset(stage, 0.0).then_inc(zero_set, 1)
            ch = Chain(dve, dve_chain)
            ch.step(V.memset(wh_w[:, :], 0.0))
            ch.step(V.memset(z_w[:, :], 0.0))
            ch.step(V.memset(wc_w[:, :], 0.0))
            ch.step(V.memset(n2_w[:, :], 0.0))
            dve.wait_ge(consts_set, 1)
            dve.wait_ge(edges_in, 16 * N_EDGE)
            V.tensor_copy(src_f[:, :], src_i[:, :]).then_inc(src_f_set, 1)
            dve.wait_ge(src_f_set, 1)
            ch.step(V.tensor_copy(dst_f[:, :], dst_i[:, :]))
            V.memset(gat_idx[:, T:T + 2 * G, :], 0)
            TS(gat_idx[:, 0:T, 0], src_f[:, :], float(N - 1), None, ALU.min)
            TS(gat_idx[:, 0:T, 1], dst_f[:, :], float(N - 1), None, ALU.min).then_inc(idx_set, 1)
            ch.step(TS(off_trash[:, :], src_f[:, :], lane[:, :], None, ALU.subtract))
            dve.wait_ge(params_in, 48)
            ch.step(TS(ew2[:, :], ew2[:, :], par[:, 4:5], par[:, 5:6], ALU.mult, ALU.add))
            ch.step(TS(tmp_b[:, :], ew2[:, :], -1.0, None, ALU.mult))
            ch.step(TT(tmp_a[:, :], ew2[:, :], tmp_b[:, :], ALU.min))
            ch.step(V.tensor_reduce(pe_[:, 4:5], par[:, 0:3], AXX, ALU.max))
            ch.step(TS(pe_[:, 0:3], par[:, 0:3], pe_[:, 4:5], None, ALU.subtract))
            ch.step(TS(pe_[:, 5:6], par[:, 3:4], -1.0, None, ALU.mult))
            TT(pe_[:, 3:4], pe_[:, 5:6], par[:, 3:4], ALU.min).then_inc(exp_in, 1)
            dve.wait_ge(exps, 2)
            ch.step(STT(tmp_b[:, :], ew2[:, :], 0.0, tmp_a[:, :], ALU.max, ALU.add))
            ch.step(TT(base[:, :], tmp_b[:, :], ew[:, :], ALU.mult))
            ch.step(TT(tmp_b[:, :], src_f[:, :], dst_f[:, :], ALU.not_equal))
            ch.step(TT(base[:, :], base[:, :], tmp_b[:, :], ALU.mult))
            ch.step(STT(pe_[:, 6:7], par[:, 3:4], 0.0, pe_[:, 3:4], ALU.max, ALU.add))
            ch.step(V.tensor_reduce(pe_[:, 5:6], pe_[:, 0:3], AXX, ALU.add))
            ch.step(V.reciprocal(pe_[:, 7:8], pe_[:, 5:6]))
            ch.step(TS(cs[:, :], pe_[:, 0:3], pe_[:, 7:8], pe_[:, 6:7], ALU.mult, ALU.mult))
            dve.wait_ge(weights_in, 16 * (N_WEIGHT - 3))

            def centre(to, of, mean):
                ch.step(V.tensor_reduce(mean, of, AXX, ALU.add))
                ch.step(TS(mean, mean, 1.0 / F, None, ALU.mult))
                ch.step(TS(to, of, mean, None, ALU.subtract))

            centre(w2c[:, :], w2x[:, :], wmean[:, :])
            centre(brow_c[:, :], brow[:, :], rmean[:, 0:1])
            centre(bn2_c[:, :], bn2_row[:, :], rmean[:, 1:2])
            ch.step(TS(zrow[:, :], brow_c[:, :], cs[:, 2:3], None, ALU.mult))
            for r in range(R):
                V.tensor_copy(zrow8[:, r, :], zrow[0:1, :])
                ch.step(V.tensor_copy(n2row8[:, r, :], bn2_c[0:1, :]))
            ch.step(TT(w2z[:, :], ident[:, 0:F], ident[:, F:P], ALU.add))
            ch.step(TS(w2z[:, :], w2z[:, :], -1.0 / F, None, ALU.add))
            ch.step(STT(w2z[:, :], w2c[:, :], cs[:, 2:3], w2z[:, :], ALU.mult, ALU.add))
            for lo, hi in ((0, F), (F, P)):
                V.tensor_copy(wh_w[lo:hi, lo:hi], w2x[lo:hi, :])
                ch.step(V.tensor_copy(z_w[lo:hi, lo:hi], w2z[lo:hi, :]))
            ch.step(V.tensor_copy(wc_w[F:P, :], w2c[F:P, :]))
            dve.wait_ge(wt_set, 1)
            for lo, hi in ((0, F), (F, P)):
                centre(n2_w[lo:hi, lo:hi], wt[lo:hi, 8, lo:hi], rmean[lo:hi, 2:3])
            V.tensor_copy(rmean[:, 2:3], rmean[:, 1:2]).then_inc(weights_set, 1)
            dve.wait_ge(weights_set, 2)
            dve.wait_ge(ef_in, 32)

            def r8(a):
                return a[:, :].rearrange("p (r f) -> p r f", f=F)

            V1, V2 = slice(NE, NE + R), slice(NE + R, NE + 2 * R)

            def bc(a, n):
                return a.unsqueeze(2).to_broadcast([P, a.shape[1], n])

            def rsqrt_step(ch, k):
                if k:
                    ch.need(ch.root)
                y, v, w = ry[:, :], rv[:, :], rw[:, :]
                if k == 0:
                    ins = TS(w.bitcast(I32), v.bitcast(I32), 1, None, ALU.logical_shift_right)
                elif k == 1:
                    ins = TS(y.bitcast(I32), w.bitcast(I32), -1.0, float(0x5F3759DF), ALU.mult, ALU.add)
                elif k % 3 == 2:
                    ins = TT(w, y, y, ALU.mult)
                elif k % 3 == 0:
                    ins = STT(w, w, -0.5, v, ALU.mult, ALU.mult)
                else:
                    ins = STT(y, w, 1.5, y, ALU.add, ALU.mult)
                ch.root = ch.mark(ins)

            ROOT_STEPS = 11

            def dense_x1(d, q):
                wait(dve, vd_set, d - 1)
                TT(r8(x1d[q]), r8(p_e), bc(ry[:, V1], F), ALU.mult).then_inc(x1d_set, 1)

            def dense_out(d):
                wait(dve, od_out, d * 16)
                TT(r8(od), r8(vd), bc(ry[:, V2], F), ALU.mult).then_inc(od_set, 1)

            def dense_v(d, q):
                wait(dve, od_ps, d + 1)
                wait(dve, od_set, d)
                TT(vd[:, :], p_o[:, :], x1d[q][:, :], ALU.add).then_inc(vd_set, 1)

            def dense_var1(d):
                wait(dve, sqd_set, d + 1)
                V.tensor_reduce(raw[:, V1], r8(sqd), AXX, ALU.add).then_inc(var1_set, 1)

            def dense_var2(d):
                wait(dve, sqv_set, d + 1)
                V.tensor_reduce(raw[:, V2], r8(sqv), AXX, ALU.add).then_inc(var2_set, 1)

            def same_src(i, q, srcb_in, done):
                wait(dve, srcb_in, i * 16 + 16)
                TT(same[q][:, :, :], srcb[:, :, :], src_f[:, grp(i)].unsqueeze(2).to_broadcast([P, G, P]),
                   ALU.is_equal).then_inc(done, 1)

            def halves(a):
                return a[:, :, :].rearrange("p g (h f) -> p (g h) f", f=F)

            def variances(ch, cols):
                return ch.mark(TS(rv[:, cols], raw[:, cols], 1.0 / F, EPS_LN, ALU.mult, ALU.add))

            ch = Chain(dve, a_chain)
            ch.step(V.memset(raw[:, :], 1.0))
            ch.step(V.memset(rv[:, :], 1.0))

            def body_a(i, q, h):
                roots = live(i - 2) or live(i - 5)
                new, old = live(i - 1), live(i - 2)

                def root(k):
                    if roots:
                        rsqrt_step(ch, k)

                if roots:
                    wait(dve, var1_set, min_int(i - 1, GROUPS))
                    wait(dve, var2_set, i - 4)
                    ch.need(variances(ch, slice(NE, NE + 2 * R)))
                root(0)
                if old:
                    wait(dve, a_sum_ps, i - 3)
                    same_src(i - 2, q, a_srcb, a_same)
                root(1)
                if new:
                    wait(dve, a_wh_ps, i)
                    wait(dve, a_sq, i - 1)
                    TT(halves(wh), r8(p_w), brow[:, :].unsqueeze(1).to_broadcast([P, R, F]), ALU.add).then_inc(a_wh, 1)
                root(2)
                if old:
                    wait(dve, a_same, i - 1)
                    t = ch.mark(TT(before[:, :, :], same[q][:, :, :],
                                   lower[:, :].unsqueeze(1).to_broadcast([P, G, P]), ALU.mult))
                root(3)
                if new:
                    ch.mark(TT(whc[1 - q][:, :, :], p_s[:, 0:G * F].rearrange("p (g f) -> p g f", f=F),
                               brow_c[:, :].unsqueeze(1).to_broadcast([P, G, F]), ALU.add))
                root(4)
                if new:
                    TT(y_all[:, grp(i - 1), :].rearrange("p g (h f) -> p (g h) f", f=F), r8(p_z),
                       zrow[:, :].unsqueeze(1).to_broadcast([P, R, F]), ALU.add).then_inc(a_y, 1)
                root(5)
                if old:
                    ch.need(t)
                    t = ch.mark(V.tensor_reduce(cnt[:, :], before[:, :, :], AXX, ALU.add))
                root(6)
                if new:
                    wait(dve, a_wh, i)
                    tp = ch.mark(TT(prod[:, :, :], wh[:, :, 0:F], wh[:, :, F:2 * F], ALU.mult))
                if old:
                    ch.need(t)
                    t = ch.mark(TS(cnt[:, :], cnt[:, :], 0.0, None, ALU.is_equal))
                root(7)
                if new:
                    ch.need(tp)
                    ch.mark(V.tensor_reduce(dot[1 - q][:, :], prod[:, :, :], AXX, ALU.add))
                if old:
                    ch.need(t)
                    t = ch.mark(TT(cnt[:, :], cnt[:, :], off_trash[:, grp(i - 2)], ALU.mult))
                root(8)
                if new:
                    wait(dve, a_sq, i)
                    V.tensor_reduce(n2[:, :, :].rearrange("p g h -> p (g h)"), halves(sq), AXX, ALU.add).then_inc(a_n2, 1)
                root(9)
                if old:
                    ch.need(t)
                    TS(sct_idx[:, grp(i - 2)], cnt[:, :], lane[:, :], None, ALU.add).then_inc(a_idx, 1)
                root(10)
                if roots:
                    ch.need(ch.root)
                if old:
                    t = ch.mark(TT(dot[q][:, :], dot[q][:, :], ry[:, 0:G], ALU.mult))
                if live(i - 5):
                    dense_out(i - 5)
                if old:
                    ch.need(t)
                    ch.mark(TS(sc1[:, :], dot[q][:, :], 0.0, cs[:, 0:1], ALU.max, ALU.mult))
                    t = ch.mark(TS(sc2[:, :], dot[q][:, :], 0.0, cs[:, 1:2], ALU.min, ALU.mult))
                if live(i - 4):
                    dense_v(i - 4, q)
                if old:
                    ch.need(t)
                    t = ch.mark(TT(sc1[:, :], sc1[:, :], sc2[:, :], ALU.add))
                    dense_x1(i - 2, q)
                    ch.need(t)
                    t = ch.mark(TT(sc1[:, :], sc1[:, :], base[:, grp(i - 2)], ALU.mult))
                if new:
                    wait(dve, a_n2, i)
                    tn = ch.mark(TT(nn[:, :], n2[:, :, 0], n2[:, :, 1], ALU.mult))
                if old:
                    ch.need(t)
                    wait(dve, a_sum_ps, i - 2)
                    TT(msg[:, :, :], whc[q][:, :, :], bc(sc1[:, :], F), ALU.mult).then_inc(a_msg, 1)
                if new:
                    ch.need(tn)
                    tn = ch.mark(TS(rv[:, 0:G], nn[:, :], EPS_SIM ** 2, None, ALU.max))
                if live(i - 4):
                    dense_var2(i - 4)
                if new:
                    dense_var1(i - 1)
                    ch.need(tn)

            over_groups(dve, GROUPS, body_a, ch, A_STEPS)

            dve.wait_ge(a_sum_ps, GROUPS)
            ch = Chain(dve, b_chain)

            def body_b(i, q, h):
                roots = live(i - 1) or live(i - 5)

                def root(k):
                    if roots:
                        rsqrt_step(ch, k)

                if roots:
                    wait(dve, b_var, min_int(i, GROUPS))
                    wait(dve, var1_set, min_int(i - 1, GROUPS) + HALF)
                    wait(dve, var2_set, i - 4 + HALF)
                    ch.need(variances(ch, slice(0, NE + 2 * R)))
                root(0)
                if live(i - 3):
                    wait(dve, b_sum_ps, i - 4)
                    same_src(i - 3, 1 - q, b_srcb, b_same)
                root(1)
                if live(i - 3):
                    wait(dve, b_m_ps, i - 3 + 1)
                    wait(dve, b_m, i - 3)
                    TT(prod[:, :, :], p_z[:, 0:G * F].rearrange("p (g f) -> p g f", f=F),
                       be2_row[:, :].unsqueeze(1).to_broadcast([P, G, F]), ALU.add).then_inc(b_m0, 1)
                for k in range(2, ROOT_STEPS):
                    root(k)
                if roots:
                    ch.need(ch.root)
                if live(i - 1):
                    wait(dve, b_keep, i - 1)
                    wait(dve, b_xt_ps, i - 1)
                    TT(halves(x1e), halves(wh), bc(ry[:, 0:NE], F), ALU.mult).then_inc(b_x1, 1)
                if live(i - 5):
                    dense_out(i - 5 + HALF)
                if live(i - 4):
                    dense_v(i - 4 + HALF, q)
                if live(i - 2):
                    dense_x1(i - 2 + HALF, q)
                if live(i):
                    wait(dve, b_pg[q], (h + 1) * (32 * G))
                    wait(dve, b_x1, i)
                    TT(wh[:, :, :], y_all[:, grp(i), :], xg[q][:, :, :], ALU.add).then_inc(b_v, 1)
                if live(i - 4):
                    dense_var2(i - 4 + HALF)
                if live(i):
                    wait(dve, b_sq, i + 1)
                    V.tensor_reduce(raw[:, 0:NE], halves(sq), AXX, ALU.add).then_inc(b_var, 1)
                if live(i - 1):
                    dense_var1(i - 1 + HALF)

            over_groups(dve, GROUPS, body_b, ch, B_STEPS)

            dve.wait_ge(b_acc, 16 * T)
            ch = Chain(dve, c_chain)

            def body_c(i, q, h):
                if live(i - 1):
                    wait(dve, c_o_ps, i)
                    ch.step(TT(prod[:, :, :], p_z[:, 0:G * F].rearrange("p (g f) -> p g f", f=F),
                               bn2_c[:, :].unsqueeze(1).to_broadcast([P, G, F]), ALU.add))
                    TT(wh[:, :, 0:F], prod[:, :, :], y_all[:, grp(i - 1), 0:F], ALU.add).then_inc(c_v, 1)
                    wait(dve, c_srcb, i * 16)
                    TT(same[0][:, :, :], srcb[:, :, :], src_f[:, grp(i - 1)].unsqueeze(2).to_broadcast([P, G, P]),
                       ALU.is_equal).then_inc(c_eq, 1)
                    wait(dve, c_sq, i)
                    V.tensor_reduce(raw[:, 0:G], sq[:, :, 0:F], AXX, ALU.add).then_inc(c_var, 1)
                    wait(dve, c_var, i)
                    ch.need(variances(ch, slice(0, NE)))
                    rsqrt_step(ch, 0)
                    t = ch.mark(V.tensor_reduce(cnt[:, :], same[0][:, :, :], AXX, ALU.add))
                    rsqrt_step(ch, 1)
                    ch.need(t)
                    t = ch.mark(TS(cnt[:, :], cnt[:, :], 0.0, float(N), ALU.is_gt, ALU.mult))
                    rsqrt_step(ch, 2)
                    ch.need(t)
                    for done in c_sct:
                        wait(dve, done, (i - 2) * (8 * G))
                    TT(si[1 - q][:, :], cnt[:, :], sct_idx[:, grp(i - 1)], ALU.max).then_inc(c_idx, 1)
                    for k in range(3, ROOT_STEPS):
                        rsqrt_step(ch, k)
                    ch.need(ch.root)
                    TT(sm[1 - q][:, :, :], wh[:, :, 0:F], bc(ry[:, 0:G], F), ALU.mult).then_inc(c_out, 1)

            over_groups(dve, GROUPS, body_c, ch, C_STEPS)


_INS = ['x', 'src', 'dst', 'edge_attr_32', 'edge_weight', 'edge_weight_n2', 'L0_gnn_W', 'L0_gnn_b',
        'L0_gnn_deg_coeff', 'L0_gnn_coeff_param', 'L0_gnn_scale_param', 'L1_gnn_We1', 'L1_gnn_be1', 'L1_gnn_We2',
        'L1_gnn_be2', 'L1_gnn_Wn1', 'L1_gnn_bn1', 'L1_gnn_Wn2', 'L1_gnn_bn2']
_OUTS = [((100000, 64), 'float32')]


A_STEPS, B_STEPS, C_STEPS = 52, 24, 30


def kernel(**inputs):
    import numpy as _np
    import concourse.bacc as _bacc
    from concourse import mybir as _mybir
    from concourse.bass_utils import run_bass_kernel_spmd as _run

    nc = _bacc.Bacc("TRN2", target_bir_lowering=False, num_devices=1)
    arrays, args = {}, []
    for name in _INS:
        a = _np.ascontiguousarray(inputs[name])
        arrays[f"in_{name}_dram"] = a
        args.append(nc.dram_tensor(f"in_{name}_dram", a.shape, _mybir.dt.from_np(a.dtype), kind="ExternalInput").ap())
    for i, (shape, dtype) in enumerate(_OUTS):
        dt = _mybir.dt.from_np(_np.dtype(dtype))
        args.append(nc.dram_tensor(f"out_{i}_dram", shape, dt, kind="ExternalOutput").ap())
    gnn(nc, *args)
    r = _run(nc, [arrays], core_ids=[0])
    return r.results[0]["out_0_dram"]
```

```python
import concourse.bass as bass
from concourse import mybir
from contextlib import ExitStack

F32 = mybir.dt.float32
I32 = mybir.dt.int32
BF16 = mybir.dt.bfloat16
ALU = mybir.AluOpType
ACT = mybir.ActivationFunctionType
AXX = mybir.AxisListType.X


class Chain:

    def __init__(self, eng, sem):
        self.eng, self.sem, self.n, self.passed = eng, sem, 0, 0

    def mark(self, ins):
        ins.then_inc(self.sem, 1)
        self.n += 1
        return self.n

    def need(self, n):
        self.eng.wait_ge(self.sem, self.passed + n)
        self.eng.nop(nofuse=True)

    def step(self, ins):
        self.need(self.mark(ins))


def wait(eng, sem, value):
    if isinstance(value, int) and value <= 0:
        return
    eng.wait_ge(sem, value)
    eng.nop(nofuse=True)


LAG = 5
A_STEPS, B_STEPS, C_STEPS = 54, 24, 30


def over_groups(eng, groups, body, chain=None, per_pass=0):
    pairs = (groups - LAG) // 2
    assert LAG + 2 * pairs == groups
    for i in range(LAG):
        body(i, i % 2, i // 2)
    n = chain.n if chain else 0
    with eng.Fori(0, pairs) as k:
        if chain:
            chain.passed = k * per_pass
        body(k * 2 + LAG, LAG % 2, k + LAG // 2)
        body(k * 2 + LAG + 1, (LAG + 1) % 2, k + (LAG + 1) // 2)
    if chain:
        assert chain.n - n == per_pass, chain.n - n
        chain.n, chain.passed = n + pairs * per_pass, 0
    for i in range(groups, groups + LAG):
        body(i, i % 2, i // 2)


def gnn(nc, x, src, dst, edge_attr, edge_w, edge_w2, W, b, deg_coeff, coeff_param, scale_param,
        We1, be1, We2, be2, Wn1, bn1, Wn2, bn2, out):
    N, F = x.shape
    E, EF = edge_attr.shape
    P = 128
    T = -(-E // P)
    G = 4
    GROUPS = T // G
    assert T == GROUPS * G
    FULL = E // T
    REST = E - FULL * T
    assert FULL == P - 1
    R = 8
    CH = P * R
    HALF = GROUPS
    B_STEP = -(-(N - CH - HALF * CH) // (HALF - 1))
    B0 = N - CH - (HALF - 1) * B_STEP
    assert B0 <= HALF * CH and B_STEP <= CH
    EPS_LN, EPS_SIM = 1e-5, 1e-8

    ZR = -(-(N + 2 * P) // (GROUPS * P)) * P
    sums = nc.dram_tensor("prop_sums", [GROUPS * ZR, F], F32, kind="Internal").ap()
    aggs = nc.dram_tensor("message_sums", [GROUPS * ZR, F], F32, kind="Internal").ap()
    src_rows = nc.dram_tensor("src_rows", [1 + T, P], F32, kind="Internal").ap()

    ctx = ExitStack()
    with ctx:
        def sb(name, shape, dt=F32):
            return ctx.enter_context(nc.sbuf_tensor(name, shape, dt))

        def ps(name):
            return ctx.enter_context(nc.psum_tensor(name, [P, 512], F32))

        def sem(name):
            return ctx.enter_context(nc.semaphore(name))

        ident = sb("ident", [P, P])
        lower = sb("lower", [P, P])
        no_src = sb("no_src", [1, P])
        lane = sb("lane", [P, G])
        wt = sb("wt", [P, 9, P])
        w2x = sb("w2x", [P, F])
        wmean = sb("wmean", [P, 1])
        w2c = sb("w2c", [P, F])
        w2z = sb("w2z", [P, F])
        wh_w = sb("wh_w", [P, P])
        wc_w = sb("wc_w", [P, F])
        z_w = sb("z_w", [P, P])
        n2_w = sb("n2_w", [P, P])
        brow = sb("brow", [P, F])
        brow_c = sb("brow_c", [P, F])
        zrow = sb("zrow", [P, F])
        be2_row = sb("be2_row", [P, F])
        bn2_row = sb("bn2_row", [P, F])
        bn2_c = sb("bn2_c", [P, F])
        PARTS = (0, 32, 64)
        ones_b = sb("ones_b", [65, P], BF16)
        rows8 = sb("rows8", [65, 2, R, F], BF16)
        part_b = sb("part_b", [P, 2, F], BF16)
        part = sb("part", [P, 2, F])
        left = sb("left", [P, 2, F])
        rmean = sb("rmean", [P, 3])
        be1_col = sb("be1_col", [F, 1])
        bn1_col = sb("bn1_col", [P, 1])
        par = sb("par", [P, 6])
        par_work = sb("par_work", [P, 8])
        warm = sb("warm", [1, 1])
        cs = sb("cs", [P, 3])
        src_i = sb("src_i", [P, T], I32)
        dst_i = sb("dst_i", [P, T], I32)
        src_f = sb("src_f", [P, T])
        dst_f = sb("dst_f", [P, T])
        base = sb("base", [P, T])
        ew = sb("ew", [P, T])
        ew2 = sb("ew2", [P, T])
        tmp_a = sb("tmp_a", [P, T])
        tmp_b = sb("tmp_b", [P, T])
        gat_idx = sb("gat_idx", [P, T + 2 * G, 2], I32)
        off_trash = sb("off_trash", [P, T])
        sct_idx = sb("sct_idx", [P, T], I32)
        ef = sb("ef", [P, T, EF])
        srct = sb("srct", [P, 2, P])
        y_all = sb("y_all", [P, T, 2 * F])
        stage = y_all[:, 0:9, :]
        gi = [sb(f"gi{q}", [P, G, 2], I32) for q in range(2)]
        si = [sb(f"si{q}", [P, G], I32) for q in range(2)]
        xg = [sb(f"xg{q}", [P, G, 2 * F]) for q in range(2)]
        xt = sb("xt", [P, G * P])
        efg = sb("efg", [P, P])
        eft = sb("eft", [P, P])
        ht = sb("ht", [F, G * P])
        srcb = sb("srcb", [P, G, P])
        same = [sb(f"same{q}", [P, G, P]) for q in range(2)]
        cross = [sb(f"cross{q}", [P, G // 2, P]) for q in range(2)]
        before = sb("before", [P, G, P])
        wh = sb("wh", [P, G, 2 * F])
        whc = [sb(f"whc{q}", [P, G, F]) for q in range(2)]
        sq = sb("sq", [P, G, 2 * F])
        prod = sb("prod", [P, G, F])
        n2 = sb("n2", [P, G, 2])
        nn = sb("nn", [P, G])
        dot = [sb(f"dot{q}", [P, G]) for q in range(2)]
        sc1 = sb("sc1", [P, G])
        sc2 = sb("sc2", [P, G])
        cnt = sb("cnt", [P, G])
        cnt_x = sb("cnt_x", [P, G // 2])
        msg = sb("msg", [P, G, F])
        x1e = sb("x1e", [P, G, 2 * F])
        sm = [sb(f"sm{q}", [P, G, F]) for q in range(2)]
        NE = 2 * G
        raw = sb("raw", [P, NE + 2 * R])
        rv = sb("rv", [P, NE + 2 * R])
        ry = sb("ry", [P, NE + 2 * R])
        rw = sb("rw", [P, NE + 2 * R])
        xd = sb("xd", [P, R * F])
        xdt = sb("xdt", [P, R * F])
        sqd = sb("sqd", [P, R * F])
        x1d = [sb(f"x1d{q}", [P, R * F]) for q in range(2)]
        x1t = sb("x1t", [P, R * F])
        hd = sb("hd", [P, R * F])
        vd = [sb(f"vd{q}", [P, R * F]) for q in range(2)]
        sqv = sb("sqv", [P, R * F])
        od = sb("od", [P, R * F])
        zero = sb("zero", [P, ZR // P * F])

        p_t, p_x, p_w, p_z, p_s, p_d, p_e, p_o = (ps(n) for n in
                                                  ("p_t", "p_x", "p_w", "p_z", "p_s", "p_d", "p_e", "p_o"))

        pads_set = sem("pads_set"); zero_set = sem("zero_set"); consts_set = sem("consts_set")
        edges_in = sem("edges_in"); params_in = sem("params_in")
        rows_in = sem("rows_in"); weights_in = sem("weights_in")
        sums_zero = sem("sums_zero"); aggs_zero = sem("aggs_zero"); ef_in = sem("ef_in")
        wt_ps = sem("wt_ps"); wt_set = sem("wt_set"); weights_set = sem("weights_set")
        srct_ps = sem("srct_ps"); srct_set = sem("srct_set"); src_rows_out = sem("src_rows_out")
        exps = sem("exps"); exp_in = sem("exp_in"); idx_set = sem("idx_set"); src_f_set = sem("src_f_set")
        dve_chain = sem("dve_chain"); pool_chain = sem("pool_chain")
        xd_in = sem("xd_in"); xd_t = sem("xd_t"); xdt_set = sem("xdt_set"); zd_ps = sem("zd_ps")
        sqd_set = sem("sqd_set"); var1_set = sem("var1_set"); x1d_set = sem("x1d_set"); x1d_t = sem("x1d_t")
        x1t_set = sem("x1t_set"); hd_ps = sem("hd_ps"); hd_set = sem("hd_set"); od_ps = sem("od_ps")
        vd_set = sem("vd_set"); sqv_set = sem("sqv_set"); var2_set = sem("var2_set")
        od_set = sem("od_set"); od_out = sem("od_out")
        a_gi = sem("a_gi"); a_xg = [sem("a_xg0"), sem("a_xg1")]
        a_srcb = sem("a_srcb"); a_same = sem("a_same"); a_idx = sem("a_idx")
        a_xt_ps = sem("a_xt_ps"); a_xt = sem("a_xt"); a_wh_ps = sem("a_wh_ps"); a_wh = sem("a_wh"); a_y = sem("a_y")
        a_sq = sem("a_sq"); a_n2 = sem("a_n2"); a_msg = sem("a_msg"); a_sum_ps = sem("a_sum_ps")
        a_sum = sem("a_sum"); a_acc = [sem("a_acc0"), sem("a_acc1")]; a_chain = sem("a_chain")
        b_gi = sem("b_gi"); b_pg = [sem("b_pg0"), sem("b_pg1")]
        b_srcb = sem("b_srcb"); b_same = sem("b_same"); b_v = sem("b_v"); b_sq = sem("b_sq"); b_var = sem("b_var")
        b_x1 = sem("b_x1"); b_ef = sem("b_ef"); b_xt_ps = sem("b_xt_ps"); b_xt = sem("b_xt"); b_keep = sem("b_keep")
        b_h_ps = sem("b_h_ps"); b_h = sem("b_h"); b_m_ps = sem("b_m_ps"); b_m0 = sem("b_m0"); b_m = sem("b_m")
        b_sum_ps = sem("b_sum_ps"); b_sum = sem("b_sum"); b_acc = [sem("b_acc0"), sem("b_acc1")]
        b_chain = sem("b_chain")
        c_gi = sem("c_gi"); c_ag = [sem("c_ag0"), sem("c_ag1")]
        c_srcb = sem("c_srcb"); c_idx = sem("c_idx"); c_eq = sem("c_eq"); c_x1 = sem("c_x1"); c_xt_ps = sem("c_xt_ps")
        c_xt = sem("c_xt"); c_h_ps = sem("c_h_ps"); c_h = sem("c_h"); c_o_ps = sem("c_o_ps"); c_v = sem("c_v")
        c_sq = sem("c_sq"); c_var = sem("c_var"); c_out = sem("c_out"); c_sct = [sem("c_sct0"), sem("c_sct1")]
        c_chain = sem("c_chain")

        def min_int(a, b):
            return min(a, b) if isinstance(a, int) else a

        def live(i):
            return not isinstance(i, int) or 0 <= i < GROUPS

        def grp(i):
            return bass.ds(i * G, G)

        def per_edge(a):
            return a[0:FULL * T].rearrange("(p t) -> p t", t=T), a[FULL * T:E].rearrange("(a t) -> a t", a=1)

        def row(a, n=P):
            return a.rearrange("(a f) -> a f", a=1).to_broadcast([n, a.shape[0]])

        def chunk(a, r0):
            return a[bass.ds(r0, CH), :].rearrange("(p r) f -> p (r f)", r=R)

        def chunk_a(i):
            return i * CH

        def chunk_b(i):
            return i * B_STEP + B0

        def store_chunk(eng, i, d0, row_of):
            if live(i - 5):
                wait(eng, od_set, i - 5 + d0 + 1)
                wait(eng, od_out, (i - 5 + d0) * 16)
                eng.dma_start(chunk(out, row_of(i - 5)), od[:, :]).then_inc(od_out, 16)

        def beside_groups(i):
            return not isinstance(i, int) or i < GROUPS

        N_EDGE, N_ROWS, N_WEIGHT = 8, 8, 11
        block = ctx.enter_context(nc.Block())

        @block.sync
        def _(sp):
            zeroed = []

            def zero_sums(pieces):
                for _ in range(min(pieces, GROUPS - len(zeroed))):
                    c = len(zeroed)
                    sp.dma_start(sums[c * ZR:(c + 1) * ZR, :].rearrange("(p r) f -> p (r f)", p=P), zero[:, :])\
                        .then_inc(sums_zero, 16)
                    zeroed.append(c)

            sp.wait_ge(zero_set, 1)
            zero_sums(1)
            sp.wait_ge(pads_set, 1)
            for a, t in ((src, src_i), (dst, dst_i), (edge_w, ew), (edge_w2, ew2)):
                whole, rest = per_edge(a)
                sp.dma_start(t[0:FULL, :], whole).then_inc(edges_in, 16)
                sp.dma_start(t[FULL:P, 0:REST], rest).then_inc(edges_in, 16)
                zero_sums(1)
            sp.dma_start(par[:, 0:3], row(coeff_param)).then_inc(params_in, 16)
            sp.dma_start(par[:, 3:4], row(scale_param)).then_inc(params_in, 16)
            sp.dma_start(par[:, 4:6], row(deg_coeff)).then_inc(params_in, 16)
            zero_sums(1)
            rows = [(w2x[0:F, :], W), (w2x[F:P, :], W),
                    (brow[:, :], row(b)), (be2_row[:, :], row(be2)), (bn2_row[:, :], row(bn2)),
                    (be1_col[:, :], be1.rearrange("(f a) -> f a", a=1)),
                    (bn1_col[0:F, :], bn1.rearrange("(f a) -> f a", a=1)),
                    (bn1_col[F:P, :], bn1.rearrange("(f a) -> f a", a=1))]
            assert len(rows) == N_ROWS
            for k, (to, of) in enumerate(rows):
                sp.dma_start(to, of).then_inc(rows_in, 16)
                if k % 3 == 0:
                    zero_sums(1)
            loads = [(stage[0:F, 0, :], We1[:, 0:P])]
            loads += [(stage[0:F, 1 + j, EF * j:EF * (j + 1)], We1[:, P:P + EF]) for j in range(G)]
            loads += [(stage[0:F, 5, 0:F], We2), (stage[0:F, 6, :], Wn1),
                      (stage[0:F, 7, 0:F], Wn1[:, 0:F]), (stage[F:P, 7, F:P], Wn1[:, 0:F]),
                      (stage[0:F, 8, 0:F], Wn2), (stage[F:P, 8, F:P], Wn2)]
            sp.wait_ge(zero_set, 2)
            for k, (to, of) in enumerate(loads):
                sp.dma_start(to, of).then_inc(weights_in, 16)
                if k % 2 == 0:
                    zero_sums(1)
            assert len(loads) == N_WEIGHT
            sp.wait_ge(srct_set, 1)
            sp.dma_start(src_rows[0:1, :], no_src[:, :]).then_inc(src_rows_out, 16)
            sp.dma_start(src_rows[1:1 + P, :], srct[:, 0, :]).then_inc(src_rows_out, 16)
            sp.dma_start(src_rows[1 + P:1 + T, :], srct[0:T - P, 1, :]).then_inc(src_rows_out, 16)
            sp.wait_ge(src_rows_out, 48)

            ef_rows = edge_attr[0:FULL * T, :].rearrange("(p t) f -> p t f", t=T)

            def load_srcb(row0, sem_in):
                sp.dma_start(srcb[:, :, :].rearrange("p g e -> p (g e)"),
                             src_rows[bass.ds(row0, G), :].rearrange("(a g) e -> a (g e)", a=1)
                             .to_broadcast([P, G * P])).then_inc(sem_in, 16)

            def load_chunk(i, d0, row_of):
                if live(i):
                    wait(sp, xd_t, i + d0)
                    sp.dma_start(xd[:, :], chunk(x, row_of(i))).then_inc(xd_in, 16)

            def body_a(i, q, h):
                load_chunk(i, 0, chunk_a)
                if live(i - 1):
                    wait(sp, a_same, i - 1)
                    load_srcb((i - 1) * G + 1, a_srcb)
                if isinstance(i, int) and i < LAG:
                    zero_sums(9)
                else:
                    sp.dma_start(ef[0:FULL, grp(i - LAG), :], ef_rows[:, grp(i - LAG), :]).then_inc(ef_in, 16)
                    sp.dma_start(aggs[bass.ds((i - LAG) * ZR, ZR), :].rearrange("(p r) f -> p (r f)", p=P), zero[:, :])\
                      .then_inc(aggs_zero, 16)
                if not beside_groups(i):
                    store_chunk(sp, i, 0, chunk_a)
                if isinstance(i, int) and i == LAG - 1:
                    assert len(zeroed) == GROUPS
                    sp.wait_ge(zero_set, 3)
                    sp.dma_start(ef[FULL:P, 0:REST, :], edge_attr[FULL * T:E, :].rearrange("(a t) f -> a t f", a=1))\
                      .then_inc(ef_in, 16)

            def body_b(i, q, h):
                load_chunk(i, HALF, chunk_b)
                if live(i - 2):
                    wait(sp, b_same, i - 2)
                    load_srcb((i - 2) * G + 1, b_srcb)
                if not beside_groups(i):
                    store_chunk(sp, i, HALF, chunk_b)

            def body_c(i, q, h):
                if live(i):
                    wait(sp, c_eq, i)
                    load_srcb(i * G, c_srcb)

            over_groups(sp, GROUPS, body_a)
            sp.wait_ge(a_same, GROUPS)
            over_groups(sp, GROUPS, body_b)
            sp.wait_ge(b_same, GROUPS)
            over_groups(sp, GROUPS, body_c)
            sp.wait_ge(od_out, 16 * 2 * HALF)

        @block.gpsimd
        def _(pool):
            ch = Chain(pool, pool_chain)
            ch.step(nc.gpsimd.memset(ident[:, :], 0.0))
            ch.step(nc.gpsimd.affine_select(out=ident[:, :], in_=ident[:, :], compare_op=ALU.not_equal, fill=1.0,
                                            base=0, pattern=[[-1, P]], channel_multiplier=1))
            ch.step(nc.gpsimd.memset(lower[:, :], 1.0))
            ch.step(nc.gpsimd.affine_select(out=lower[:, :], in_=lower[:, :], compare_op=ALU.is_gt, fill=0.0,
                                            base=0, pattern=[[-1, P]], channel_multiplier=1))
            ch.step(nc.gpsimd.iota(lane[:, :], pattern=[[0, G // 2], [P, 2]], base=N, channel_multiplier=1,
                                   allow_small_or_imprecise_dtypes=True))
            nc.gpsimd.memset(no_src[:, :], -1.0).then_inc(consts_set, 1)

            def gather(to, table, index, done):
                nc.gpsimd.indirect_dma_start(to, None, table, bass.IndirectOffsetOnAxis(ap=index, axis=0))\
                    .then_inc(done, 16)

            def add(table, q, j, tile, acc):
                if j % 2 == 0:
                    wait(pool, acc[0], tile * 8)
                    wait(pool, acc[1], tile * 8)
                nc.gpsimd.indirect_dma_start(table, bass.IndirectOffsetOnAxis(ap=si[q][:, j:j + 1], axis=0),
                                             sm[q][:, j, :], None, compute_op=ALU.add).then_inc(acc[j % 2], 16)

            def gather_both(table, q, j, done):
                gather(xg[q][:, j, 0:F], table, gi[q][:, j, 0:1], done[q])
                gather(xg[q][:, j, F:2 * F], table, gi[q][:, j, 1:2], done[q])

            def adds(table, i, q, half, ready, acc):
                lag, pair = (5, 1) if half == 0 else (4, 0)
                if live(i - lag):
                    wait(pool, ready, i - lag + 1)
                    for j in (2 * pair, 2 * pair + 1):
                        add(table, (q + lag) % 2, j, (i - lag) * G + j, acc)

            def body_a(i, q, h):
                if live(i):
                    wait(pool, a_gi, i + 1)
                    wait(pool, a_xt_ps, i - 1)
                for half in range(2):
                    if live(i):
                        for j in (2 * half, 2 * half + 1):
                            gather_both(x, q, j, a_xg)
                    if isinstance(i, int) and i == 4 and half == 1:
                        pool.wait_ge(sums_zero, 16 * GROUPS)
                    adds(sums, i, q, half, a_sum, a_acc)

            over_groups(pool, GROUPS, body_a)
            for done in a_acc:
                pool.wait_ge(done, 8 * T)

            def body_b(i, q, h):
                if live(i):
                    wait(pool, b_gi, i + 1)
                    wait(pool, b_v, i - 1)
                for half in range(2):
                    if live(i):
                        for j in (2 * half, 2 * half + 1):
                            gather_both(sums, q, j, b_pg)
                    if isinstance(i, int) and i == 4 and half == 1:
                        pool.wait_ge(aggs_zero, 16 * GROUPS)
                    adds(aggs, i, q, half, b_sum, b_acc)

            over_groups(pool, GROUPS, body_b)
            for done in b_acc:
                pool.wait_ge(done, 8 * T)

            def body_c(i, q, h):
                if live(i):
                    wait(pool, c_gi, i + 1)
                    wait(pool, c_xt_ps, i - 1)
                if live(i - 3):
                    wait(pool, c_out, i - 3 + 1)
                    wait(pool, c_idx, i - 3 + 1)
                for j in range(G):
                    if live(i):
                        gather(xg[q][:, j, F:2 * F], aggs, gi[q][:, j, 0:1], c_ag[q])
                    if live(i - 3):
                        wait(pool, c_sct[j % 2], ((i - 3) * (G // 2) + j // 2) * 16)
                        nc.gpsimd.indirect_dma_start(out, bass.IndirectOffsetOnAxis(ap=si[1 - q][:, j:j + 1], axis=0),
                                                     sm[1 - q][:, j, :], None, bounds_check=N - 1, oob_is_err=False)\
                            .then_inc(c_sct[j % 2], 16)
                if isinstance(i, int) and i == 2:
                    pool.wait_ge(od_out, 16 * 2 * HALF)

            over_groups(pool, GROUPS, body_c)
            for done in c_sct:
                pool.wait_ge(done, 16 * T // 2)

        @block.tensor
        def _(pe):
            mm, tr = nc.tensor.matmul, nc.tensor.transpose

            pe.wait_ge(consts_set, 1)
            pe.wait_ge(src_f_set, 1)
            tr(p_t[:, 0:P], src_f[:, 0:P], ident[:, :])
            tr(p_t[0:T - P, P:2 * P], src_f[:, P:T], ident[:, :]).then_inc(srct_ps, 1)
            pe.wait_ge(weights_in, 16 * N_WEIGHT)
            for k in range(9):
                last = tr((p_w, p_z, p_s)[k // 4][:, (k % 4) * P:(k % 4 + 1) * P], stage[:, k, :], ident[:, :])
            last.then_inc(wt_ps, 1)
            pe.wait_ge(weights_set, 1)
            pe.wait_ge(wt_set, 1)

            def dense_in(d):
                wait(pe, xd_in, d * 16 + 16)
                wait(pe, xdt_set, d)
                for k in range(4):
                    last = tr(p_d[:, k * P:(k + 1) * P], xd[:, k * P:(k + 1) * P], ident[:, :])
                last.then_inc(xd_t, 1)

            def with_row(p, left, right, biases):
                mm(p[:, :], ones_b[:, :], biases.rearrange("a r f -> a (r f)"), start=True, stop=False)
                for k in range(4):
                    s = slice(k * P, (k + 1) * P)
                    last = mm(p[:, s], left[:, s], right, start=False, stop=k == 3)
                return last

            def dense_z(d):
                wait(pe, xdt_set, d + 1)
                wait(pe, x1d_set, d)
                with_row(p_e, xdt, z_w[:, :], rows8[:, 0, :, :]).then_inc(zd_ps, 1)

            def dense_t(d, q):
                wait(pe, x1d_set, d + 1)
                wait(pe, x1t_set, d)
                for k in range(4):
                    last = tr(p_x[:, k * P:(k + 1) * P], x1d[q][:, k * P:(k + 1) * P], ident[:, :])
                last.then_inc(x1d_t, 1)

            def dense_h(d):
                wait(pe, x1t_set, d + 1)
                mm(p_t[:, :], wt[:, 7, :], x1t[:, :], start=True, stop=True).then_inc(hd_ps, 1)

            def dense_o(d):
                wait(pe, hd_set, d + 1)
                wait(pe, vd_set, d)
                with_row(p_o, hd, n2_w[:, :], rows8[:, 1, :, :]).then_inc(od_ps, 1)

            def group_sum(p, q, done):
                for j in range(G):
                    s = slice(j * F, (j + 1) * F)
                    last = mm(p[:, s], same[q][:, j, :], msg[:, j, :], start=True, stop=j % 2 == 1)
                    if j % 2 == 0:
                        last = mm(p[:, s], cross[q][:, j // 2, :], msg[:, j + 1, :], start=False, stop=True)
                last.then_inc(done, 1)

            def body_a(i, q, h):
                d = i - 3
                if live(i):
                    wait(pe, a_xt, i)
                    wait(pe, hd_set, i - 3)
                    wait(pe, a_xg[q], (h + 1) * (32 * G))
                    for j in range(G):
                        last = tr(p_t[:, j * P:(j + 1) * P], xg[q][:, j, :], ident[:, :])
                    last.then_inc(a_xt_ps, 1)
                if live(d):
                    wait(pe, a_sum, i - 3)
                    dense_t(d, 1 - q)
                if live(i):
                    dense_in(i)
                if live(d):
                    wait(pe, a_xt, min_int(i + 1, GROUPS))
                    dense_h(d)
                    wait(pe, a_msg, i - 3 + 1)
                    wait(pe, a_same, i - 3 + 1)
                    group_sum(p_x, 1 - q, a_sum_ps)
                if live(i):
                    wait(pe, a_xt, i + 1)
                    wait(pe, a_wh, i)
                    wait(pe, a_y, i)
                    for j in range(G):
                        lhs = xt[:, j * P:(j + 1) * P]
                        mm(p_w[:, j * P:(j + 1) * P], lhs, wh_w[:, :], start=True, stop=True)
                        mm(p_z[:, j * P:(j + 1) * P], lhs, z_w[:, :], start=True, stop=True)
                        last = mm(p_s[:, j * F:(j + 1) * F], lhs, wc_w[:, :], start=True, stop=True)
                    last.then_inc(a_wh_ps, 1)
                if isinstance(i, int) and i == 1:
                    pe.wait_ge(weights_set, 2)
                if live(i - 1):
                    dense_z(i - 1)
                if live(d):
                    dense_o(d)

            def body_b(i, q, h):
                g, d = i - 2, i - 3 + HALF
                if live(g):
                    wait(pe, b_x1, g + 1)
                    wait(pe, hd_set, d)
                    for j in range(G):
                        tr(p_t[:, j * P:(j + 1) * P], x1e[:, j, :], ident[:, :])
                    wait(pe, b_ef, g + 1)
                    wait(pe, x1t_set, min_int(d, 2 * HALF))
                    tr(p_x[:, 0:P], efg[:, :], ident[:, :]).then_inc(b_xt_ps, 1)
                if live(i):
                    dense_in(i + HALF)
                if live(i - 3):
                    wait(pe, b_xt, min_int(g + 1, GROUPS))
                    dense_t(d, 1 - q)
                    wait(pe, b_m, i - 3 + 1)
                    wait(pe, b_same, i - 3 + 1)
                    wait(pe, b_sum, i - 3)
                    group_sum(p_s, 1 - q, b_sum_ps)
                if live(g):
                    wait(pe, b_xt, g + 1)
                    wait(pe, b_h, g)
                    for j in range(G):
                        s = slice(j * P, (j + 1) * P)
                        mm(p_w[0:F, s], wt[:, 0, 0:F], xt[:, s], start=True, stop=False)
                        last = mm(p_w[0:F, s], wt[:, 1 + j, 0:F], eft[:, :], start=False, stop=True)
                    last.then_inc(b_h_ps, 1)
                if live(i - 3):
                    dense_h(d)
                if live(i - 1):
                    dense_z(i - 1 + HALF)
                if live(g):
                    wait(pe, b_h, g + 1)
                    wait(pe, b_m0, g)
                    for j in range(G):
                        last = mm(p_z[:, j * F:(j + 1) * F], ht[:, j * P:(j + 1) * P], wt[0:F, 5, 0:F],
                                  start=True, stop=True)
                    last.then_inc(b_m_ps, 1)
                if live(i - 3):
                    dense_o(d)

            def body_c(i, q, h):
                if live(i):
                    wait(pe, c_ag[q], (h + 1) * (16 * G))
                    wait(pe, c_x1, i + 1)
                    wait(pe, c_xt, i)
                    for j in range(G):
                        last = tr(p_t[:, j * P:(j + 1) * P], xg[q][:, j, :], ident[:, :])
                    last.then_inc(c_xt_ps, 1)
                    wait(pe, c_xt, i + 1)
                    wait(pe, c_h, i)
                    mm(p_w[0:F, :], wt[:, 6, 0:F], xt[:, :], start=True, stop=True).then_inc(c_h_ps, 1)
                    wait(pe, c_h, i + 1)
                    wait(pe, c_v, i)
                    for j in range(G):
                        last = mm(p_z[:, j * F:(j + 1) * F], ht[:, j * P:(j + 1) * P], n2_w[0:F, 0:F],
                                  start=True, stop=True)
                    last.then_inc(c_o_ps, 1)

            over_groups(pe, GROUPS, body_a)
            over_groups(pe, GROUPS, body_b)
            over_groups(pe, GROUPS, body_c)

        @block.scalar
        def _(act):
            A = nc.scalar.activation

            def copy_gi(i, q, done):
                nc.scalar.copy(gi[q][:, :, :], gat_idx[:, grp(i), :]).then_inc(done, 1)

            def first_gi(done):
                copy_gi(0, 0, done)
                copy_gi(1, 1, done)

            act.wait_ge(idx_set, 1)
            first_gi(a_gi)
            act.wait_ge(exp_in, 1)
            A(par_work[:, 0:4], par_work[:, 0:4], ACT.Exp)
            A(tmp_a[:, :], tmp_a[:, :], ACT.Exp).then_inc(exps, 1)
            act.wait_ge(exps, 1)
            A(par_work[:, 3:4], par_work[:, 3:4], ACT.Ln, bias=1.0)
            A(tmp_a[:, :], tmp_a[:, :], ACT.Ln, bias=1.0).then_inc(exps, 1)
            act.wait_ge(exps, 2)
            A(warm[:, :], par_work[0:1, 3:4], ACT.Silu)
            act.wait_ge(srct_ps, 1)
            nc.scalar.copy(srct[:, 0, :], p_t[:, 0:P])
            nc.scalar.copy(srct[0:T - P, 1, :], p_t[0:T - P, P:2 * P]).then_inc(srct_set, 1)
            act.wait_ge(wt_ps, 1)
            nc.scalar.copy(wt[:, 0:4, :].rearrange("p k f -> p (k f)"), p_w[:, :])
            nc.scalar.copy(wt[:, 4:8, :].rearrange("p k f -> p (k f)"), p_z[:, :])
            nc.scalar.copy(wt[:, 8, :], p_s[:, 0:P]).then_inc(wt_set, 1)

            def dense_xt(d):
                wait(act, xd_t, d + 1)
                wait(act, zd_ps, d)
                nc.scalar.copy(xdt[:, :], p_d[:, :]).then_inc(xdt_set, 1)

            def dense_sq(d):
                wait(act, zd_ps, d + 1)
                wait(act, var1_set, d)
                A(sqd[:, :], p_e[:, :], ACT.Square).then_inc(sqd_set, 1)

            def dense_x1t(d):
                wait(act, x1d_t, d + 1)
                wait(act, hd_ps, d)
                nc.scalar.copy(x1t[:, :], p_x[:, :]).then_inc(x1t_set, 1)

            def dense_silu(d):
                wait(act, hd_ps, d + 1)
                wait(act, od_ps, d)
                A(hd[:, :], p_t[:, :], ACT.Silu, bias=bn1_col[:, :]).then_inc(hd_set, 1)

            def dense_sqv(d, q):
                wait(act, vd_set, d + 1)
                wait(act, var2_set, d)
                A(sqv[:, :], vd[q][:, :], ACT.Square).then_inc(sqv_set, 1)

            def keep_sum(p, g, q, sum_ps, acc, done):
                wait(act, sum_ps, g + 1)
                for done_tiles in acc:
                    wait(act, done_tiles, (g - 1) * (8 * G))
                nc.scalar.copy(si[q][:, :], sct_idx[:, grp(g)])
                nc.scalar.copy(sm[q][:, :, :].rearrange("p g f -> p (g f)"), p[:, 0:G * F]).then_inc(done, 1)

            def body_a(i, q, h):
                if live(i):
                    wait(act, a_xt_ps, i + 1)
                    wait(act, a_wh_ps, i)
                    nc.scalar.copy(xt[:, :], p_t[:, :]).then_inc(a_xt, 1)
                    copy_gi(i + 2, q, a_gi)
                if live(i - 3):
                    dense_x1t(i - 3)
                if live(i - 1):
                    wait(act, a_wh, i)
                    wait(act, a_n2, i - 1)
                    A(sq[:, :, :], wh[:, :, :], ACT.Square).then_inc(a_sq, 1)
                if live(i - 3):
                    dense_silu(i - 3)
                    wait(act, a_idx, i - 3 + 1)
                    keep_sum(p_x, i - 3, 1 - q, a_sum_ps, a_acc, a_sum)
                if live(i - 4):
                    dense_sqv(i - 4, q)
                if live(i - 1):
                    dense_sq(i - 1)
                if live(i):
                    dense_xt(i)
                if beside_groups(i):
                    store_chunk(act, i, 0, chunk_a)

            def body_b(i, q, h):
                g = i - 2
                if live(i - 1):
                    wait(act, b_xt_ps, i - 1)
                    nc.scalar.copy(efg[:, :], ef[:, grp(i - 1), :].rearrange("p g f -> p (g f)")).then_inc(b_ef, 1)
                if live(g):
                    wait(act, b_xt_ps, g + 1)
                    wait(act, b_h_ps, g)
                    nc.scalar.copy(xt[:, :], p_t[:, :])
                    nc.scalar.copy(eft[:, :], p_x[:, 0:P]).then_inc(b_xt, 1)
                    nc.scalar.copy(y_all[:, grp(g), 0:F], x1e[:, :, 0:F]).then_inc(b_keep, 1)
                if live(i - 3):
                    dense_x1t(i - 3 + HALF)
                    wait(act, b_m0, i - 3 + 1)
                    wait(act, b_sum_ps, i - 3)
                    A(msg[:, :, :], prod[:, :, :], ACT.Silu).then_inc(b_m, 1)
                    keep_sum(p_s, i - 3, 1 - q, b_sum_ps, b_acc, b_sum)
                if live(g):
                    wait(act, b_h_ps, g + 1)
                    wait(act, b_m_ps, g)
                    A(ht[:, :], p_w[0:F, :], ACT.Silu, bias=be1_col[:, :]).then_inc(b_h, 1)
                if live(i - 3):
                    dense_silu(i - 3 + HALF)
                if live(i - 4):
                    dense_sqv(i - 4 + HALF, q)
                if live(i):
                    wait(act, b_v, i + 1)
                    wait(act, b_var, i)
                    A(sq[:, :, :], wh[:, :, :], ACT.Square).then_inc(b_sq, 1)
                    copy_gi(i + 2, q, b_gi)
                if live(i - 1):
                    dense_sq(i - 1 + HALF)
                if live(i):
                    dense_xt(i + HALF)
                if beside_groups(i):
                    store_chunk(act, i, HALF, chunk_b)

            def body_c(i, q, h):
                if live(i):
                    wait(act, c_xt_ps, i - 1)
                    nc.scalar.copy(xg[q][:, :, 0:F], y_all[:, grp(i), 0:F]).then_inc(c_x1, 1)
                if live(i - 1):
                    wait(act, c_v, i)
                    wait(act, c_var, i - 1)
                    A(sq[:, :, 0:F], wh[:, :, 0:F], ACT.Square).then_inc(c_sq, 1)
                if live(i):
                    wait(act, c_xt_ps, i + 1)
                    wait(act, c_h_ps, i)
                    nc.scalar.copy(xt[:, :], p_t[:, :]).then_inc(c_xt, 1)
                    wait(act, c_h_ps, i + 1)
                    wait(act, c_o_ps, i)
                    A(ht[:, :], p_w[0:F, :], ACT.Silu, bias=bn1_col[0:F, :]).then_inc(c_h, 1)
                    copy_gi(i + 2, q, c_gi)

            over_groups(act, GROUPS, body_a)
            first_gi(b_gi)
            for done in a_acc:
                act.wait_ge(done, 8 * T)
            act.wait_ge(ef_in, 16 * (GROUPS + 1))
            over_groups(act, GROUPS, body_b)
            first_gi(c_gi)
            for done in b_acc:
                act.wait_ge(done, 8 * T)
            over_groups(act, GROUPS, body_c)

        @block.vector
        def _(dve):
            V = nc.vector
            TT, TS, STT = V.tensor_tensor, V.tensor_scalar, V.scalar_tensor_tensor
            V.memset(zero[:, :], 0.0).then_inc(zero_set, 1)
            V.memset(src_i[96:P, :], N + P - 1)
            V.memset(dst_i[96:P, :], 0)
            V.memset(ew[96:P, :], 0.0)
            V.memset(ew2[96:P, :], 0.0).then_inc(pads_set, 1)
            V.memset(stage, 0.0).then_inc(zero_set, 1)
            ch = Chain(dve, dve_chain)
            ch.step(V.memset(wh_w[:, :], 0.0))
            ch.step(V.memset(z_w[:, :], 0.0))
            ch.step(V.memset(wc_w[:, :], 0.0))
            ch.step(V.memset(n2_w[:, :], 0.0))
            V.memset(ones_b[:, :], 1.0)
            ch.step(V.memset(rows8[:, :, :, :], 0.0))
            dve.wait_ge(consts_set, 1)
            dve.wait_ge(edges_in, 16 * N_EDGE)
            V.tensor_copy(src_f[:, :], src_i[:, :]).then_inc(src_f_set, 1)
            dve.wait_ge(src_f_set, 1)
            ch.step(V.tensor_copy(dst_f[:, :], dst_i[:, :]))
            V.memset(gat_idx[:, T:T + 2 * G, :], 0)
            TS(gat_idx[:, 0:T, 0], src_f[:, :], float(N - 1), None, ALU.min)
            TS(gat_idx[:, 0:T, 1], dst_f[:, :], float(N - 1), None, ALU.min).then_inc(idx_set, 1)
            ch.step(TT(off_trash[:, :].rearrange("p (k g) -> p k g", g=G),
                       src_f[:, :].rearrange("p (k g) -> p k g", g=G),
                       lane[:, :].unsqueeze(1).to_broadcast([P, GROUPS, G]), ALU.subtract))
            dve.wait_ge(params_in, 48)
            ch.step(TS(ew2[:, :], ew2[:, :], par[:, 4:5], par[:, 5:6], ALU.mult, ALU.add))
            ch.step(TS(tmp_b[:, :], ew2[:, :], -1.0, None, ALU.mult))
            ch.step(TT(tmp_a[:, :], ew2[:, :], tmp_b[:, :], ALU.min))
            ch.step(V.tensor_reduce(par_work[:, 4:5], par[:, 0:3], AXX, ALU.max))
            ch.step(TS(par_work[:, 0:3], par[:, 0:3], par_work[:, 4:5], None, ALU.subtract))
            ch.step(TS(par_work[:, 5:6], par[:, 3:4], -1.0, None, ALU.mult))
            TT(par_work[:, 3:4], par_work[:, 5:6], par[:, 3:4], ALU.min).then_inc(exp_in, 1)
            dve.wait_ge(exps, 2)
            ch.step(STT(tmp_b[:, :], ew2[:, :], 0.0, tmp_a[:, :], ALU.max, ALU.add))
            ch.step(TT(base[:, :], tmp_b[:, :], ew[:, :], ALU.mult))
            ch.step(TT(tmp_b[:, :], src_f[:, :], dst_f[:, :], ALU.not_equal))
            ch.step(TT(base[:, :], base[:, :], tmp_b[:, :], ALU.mult))
            ch.step(STT(par_work[:, 6:7], par[:, 3:4], 0.0, par_work[:, 3:4], ALU.max, ALU.add))
            ch.step(V.tensor_reduce(par_work[:, 5:6], par_work[:, 0:3], AXX, ALU.add))
            ch.step(V.reciprocal(par_work[:, 7:8], par_work[:, 5:6]))
            ch.step(TS(cs[:, :], par_work[:, 0:3], par_work[:, 7:8], par_work[:, 6:7], ALU.mult, ALU.mult))
            dve.wait_ge(rows_in, 16 * N_ROWS)
            centred = ((w2c, w2x, wmean[:, :]), (brow_c, brow, rmean[:, 0:1]), (bn2_c, bn2_row, rmean[:, 1:2]))
            for _, of, mean in centred:
                t = ch.mark(V.tensor_reduce(mean, of[:, :], AXX, ALU.add))
            ch.need(t)
            for _, _, mean in centred:
                t = ch.mark(TS(mean, mean, 1.0 / F, None, ALU.mult))
            ch.need(t)
            for to, of, mean in centred:
                ch.mark(TS(to[:, :], of[:, :], mean, None, ALU.subtract))
            ch.step(TT(w2z[:, :], ident[:, 0:F], ident[:, F:P], ALU.add))
            ch.mark(TS(zrow[:, :], brow_c[:, :], cs[:, 2:3], None, ALU.mult))
            ch.step(TS(w2z[:, :], w2z[:, :], -1.0 / F, None, ALU.add))
            for lo, hi in ((0, F), (F, P)):
                ch.mark(V.tensor_copy(wh_w[lo:hi, lo:hi], w2x[lo:hi, :]))
            ch.step(STT(w2z[:, :], w2c[:, :], cs[:, 2:3], w2z[:, :], ALU.mult, ALU.add))
            ch.mark(V.tensor_copy(wc_w[F:P, :], w2c[F:P, :]))
            V.tensor_copy(z_w[0:F, 0:F], w2z[0:F, :])
            V.tensor_copy(z_w[F:P, F:P], w2z[F:P, :]).then_inc(weights_set, 1)
            V.tensor_copy(left[:, 0, :], zrow[:, :])
            ch.step(V.tensor_copy(left[:, 1, :], bn2_c[:, :]))
            for k, p0 in enumerate(PARTS):
                ch.mark(V.tensor_copy(rows8[p0:p0 + 1, :, :, :],
                                      left[p0:p0 + 1, :, :].unsqueeze(2).to_broadcast([1, 2, R, F])))
                if k < 2:
                    ch.step(V.tensor_copy(part_b[:, :, :], left[:, :, :]))
                    ch.step(V.tensor_copy(part[:, :, :], part_b[:, :, :]))
                    ch.step(TT(left[:, :, :], left[:, :, :], part[:, :, :], ALU.subtract))
            dve.wait_ge(wt_set, 1)
            ch.step(V.tensor_reduce(rmean[:, 2:3], wt[:, 8, :], AXX, ALU.add))
            ch.step(TS(rmean[:, 2:3], rmean[:, 2:3], 1.0 / F, None, ALU.mult))
            TS(n2_w[0:F, 0:F], wt[0:F, 8, 0:F], rmean[0:F, 2:3], None, ALU.subtract)
            TS(n2_w[F:P, F:P], wt[F:P, 8, F:P], rmean[F:P, 2:3], None, ALU.subtract).then_inc(weights_set, 1)
            dve.wait_ge(weights_set, 2)
            V.memset(ef[96:P, REST:T, :], 0.0).then_inc(zero_set, 1)

            def r8(a):
                return a[:, :].rearrange("p (r f) -> p r f", f=F)

            V1, V2 = slice(NE, NE + R), slice(NE + R, NE + 2 * R)

            def bc(a, n):
                return a.unsqueeze(2).to_broadcast([P, a.shape[1], n])

            def rsqrt_step(ch, k):
                if k:
                    ch.need(ch.root)
                y, v, w = ry[:, :], rv[:, :], rw[:, :]
                if k == 0:
                    ins = TS(w.bitcast(I32), v.bitcast(I32), 1, None, ALU.logical_shift_right)
                elif k == 1:
                    ins = TS(y.bitcast(I32), w.bitcast(I32), -1.0, float(0x5F3759DF), ALU.mult, ALU.add)
                elif k % 3 == 2:
                    ins = TT(w, y, y, ALU.mult)
                elif k % 3 == 0:
                    ins = STT(w, w, -0.5, v, ALU.mult, ALU.mult)
                else:
                    ins = STT(y, w, 1.5, y, ALU.add, ALU.mult)
                ch.root = ch.mark(ins)

            ROOT_STEPS = 11

            def dense_x1(d, q):
                wait(dve, vd_set, d - 1)
                TT(r8(x1d[q]), r8(p_e), bc(ry[:, V1], F), ALU.mult).then_inc(x1d_set, 1)

            def dense_out(d, q):
                wait(dve, od_out, d * 16)
                TT(r8(od), r8(vd[q]), bc(ry[:, V2], F), ALU.mult).then_inc(od_set, 1)

            def dense_v(d, q):
                wait(dve, od_ps, d + 1)
                wait(dve, od_set, d - 1)
                TT(vd[q][:, :], p_o[:, :], x1d[q][:, :], ALU.add).then_inc(vd_set, 1)

            def dense_var1(d):
                wait(dve, sqd_set, d + 1)
                V.tensor_reduce(raw[:, V1], r8(sqd), AXX, ALU.add).then_inc(var1_set, 1)

            def dense_var2(d):
                wait(dve, sqv_set, d + 1)
                V.tensor_reduce(raw[:, V2], r8(sqv), AXX, ALU.add).then_inc(var2_set, 1)

            def same_src(i, q, srcb_in):
                wait(dve, srcb_in, i * 16 + 16)
                TT(same[q][:, :, :], srcb[:, :, :], src_f[:, grp(i)].unsqueeze(2).to_broadcast([P, G, P]),
                   ALU.is_equal)

            def cross_src(i, q, done):
                TT(cross[q][:, :, :], srcb[:, :, :].rearrange("p (k two) e -> p k two e", two=2)[:, :, 0, :],
                   odd(src_f[:, grp(i)]).unsqueeze(2).to_broadcast([P, G // 2, P]), ALU.is_equal).then_inc(done, 1)

            def odd(a):
                return a.rearrange("p (k two) -> p k two", two=2)[:, :, 1]

            def halves(a):
                return a[:, :, :].rearrange("p g (h f) -> p (g h) f", f=F)

            def variances(ch, cols):
                return ch.mark(TS(rv[:, cols], raw[:, cols], 1.0 / F, EPS_LN, ALU.mult, ALU.add))

            ch = Chain(dve, a_chain)
            ch.step(V.memset(raw[:, :], 1.0))
            ch.step(V.memset(rv[:, :], 1.0))

            def body_a(i, q, h):
                roots = live(i - 2) or live(i - 5)
                new, old = live(i - 1), live(i - 2)

                def root(k):
                    if roots:
                        rsqrt_step(ch, k)

                if roots:
                    wait(dve, var1_set, min_int(i - 1, GROUPS))
                    wait(dve, var2_set, i - 4)
                    t_var = variances(ch, slice(NE, NE + 2 * R))
                if old:
                    wait(dve, a_sum_ps, i - 3)
                    same_src(i - 2, q, a_srcb)
                if roots:
                    ch.need(t_var)
                root(0)
                if old:
                    cross_src(i - 2, q, a_same)
                root(1)
                if new:
                    wait(dve, a_wh_ps, i)
                    wait(dve, a_sq, i - 1)
                    TT(halves(wh), r8(p_w), brow[:, :].unsqueeze(1).to_broadcast([P, R, F]), ALU.add).then_inc(a_wh, 1)
                root(2)
                if old:
                    wait(dve, a_same, i - 1)
                    t = ch.mark(TT(before[:, :, :], same[q][:, :, :],
                                   lower[:, :].unsqueeze(1).to_broadcast([P, G, P]), ALU.mult))
                root(3)
                if new:
                    ch.mark(TT(whc[1 - q][:, :, :], p_s[:, 0:G * F].rearrange("p (g f) -> p g f", f=F),
                               brow_c[:, :].unsqueeze(1).to_broadcast([P, G, F]), ALU.add))
                root(4)
                if new:
                    TT(y_all[:, grp(i - 1), :].rearrange("p g (h f) -> p (g h) f", f=F), r8(p_z),
                       zrow[:, :].unsqueeze(1).to_broadcast([P, R, F]), ALU.add).then_inc(a_y, 1)
                root(5)
                if old:
                    ch.need(t)
                    ch.mark(V.tensor_reduce(cnt_x[:, :], cross[q][:, :, :], AXX, ALU.add))
                    t = ch.mark(V.tensor_reduce(cnt[:, :], before[:, :, :], AXX, ALU.add))
                root(6)
                if new:
                    wait(dve, a_wh, i)
                    tp = ch.mark(TT(prod[:, :, :], wh[:, :, 0:F], wh[:, :, F:2 * F], ALU.mult))
                if old:
                    ch.need(t)
                    t = ch.mark(TT(odd(cnt[:, :]), odd(cnt[:, :]), cnt_x[:, :], ALU.add))
                root(7)
                if new:
                    ch.need(tp)
                    ch.mark(V.tensor_reduce(dot[1 - q][:, :], prod[:, :, :], AXX, ALU.add))
                if old:
                    ch.need(t)
                    t = ch.mark(STT(cnt[:, :], cnt[:, :], 0.0, off_trash[:, grp(i - 2)], ALU.is_equal, ALU.mult))
                root(8)
                if live(i - 4):
                    dense_v(i - 4, q)
                root(9)
                if new:
                    wait(dve, a_sq, i)
                    V.tensor_reduce(n2[:, :, :].rearrange("p g h -> p (g h)"), halves(sq), AXX, ALU.add)\
                        .then_inc(a_n2, 1)
                root(10)
                if old:
                    ch.need(t)
                    TT(sct_idx[:, grp(i - 2)], cnt[:, :], lane[:, :], ALU.add).then_inc(a_idx, 1)
                if roots:
                    ch.need(ch.root)
                if old:
                    t = ch.mark(TT(dot[q][:, :], dot[q][:, :], ry[:, 0:G], ALU.mult))
                if live(i - 2):
                    dense_x1(i - 2, q)
                if old:
                    ch.need(t)
                    ch.mark(TS(sc1[:, :], dot[q][:, :], 0.0, cs[:, 0:1], ALU.max, ALU.mult))
                    t = ch.mark(TS(sc2[:, :], dot[q][:, :], 0.0, cs[:, 1:2], ALU.min, ALU.mult))
                if live(i - 5):
                    dense_out(i - 5, 1 - q)
                if old:
                    ch.need(t)
                    t = ch.mark(TT(sc1[:, :], sc1[:, :], sc2[:, :], ALU.add))
                if new:
                    wait(dve, a_n2, i)
                    tn = ch.mark(TT(nn[:, :], n2[:, :, 0], n2[:, :, 1], ALU.mult))
                if old:
                    ch.need(t)
                    t = ch.mark(TT(sc1[:, :], sc1[:, :], base[:, grp(i - 2)], ALU.mult))
                if live(i - 4):
                    dense_var2(i - 4)
                if old:
                    ch.need(t)
                    wait(dve, a_sum_ps, i - 2)
                    TT(msg[:, :, :], whc[q][:, :, :], bc(sc1[:, :], F), ALU.mult).then_inc(a_msg, 1)
                if new:
                    ch.need(tn)
                    tn = ch.mark(TS(rv[:, 0:G], nn[:, :], EPS_SIM ** 2, None, ALU.max))
                    dense_var1(i - 1)
                    ch.need(tn)

            over_groups(dve, GROUPS, body_a, ch, A_STEPS)

            dve.wait_ge(a_sum_ps, GROUPS)
            ch = Chain(dve, b_chain)

            def body_b(i, q, h):
                roots = live(i - 1) or live(i - 5)

                def root(k):
                    if roots:
                        rsqrt_step(ch, k)

                if roots:
                    wait(dve, b_var, min_int(i, GROUPS))
                    wait(dve, var1_set, min_int(i - 1, GROUPS) + HALF)
                    wait(dve, var2_set, i - 4 + HALF)
                    t_var = variances(ch, slice(0, NE + 2 * R))
                if live(i - 3):
                    wait(dve, b_sum_ps, i - 4)
                    same_src(i - 3, 1 - q, b_srcb)
                if roots:
                    ch.need(t_var)
                root(0)
                if live(i - 3):
                    cross_src(i - 3, 1 - q, b_same)
                root(1)
                if live(i - 3):
                    wait(dve, b_m_ps, i - 3 + 1)
                    wait(dve, b_m, i - 3)
                    TT(prod[:, :, :], p_z[:, 0:G * F].rearrange("p (g f) -> p g f", f=F),
                       be2_row[:, :].unsqueeze(1).to_broadcast([P, G, F]), ALU.add).then_inc(b_m0, 1)
                root(2)
                if live(i - 4):
                    dense_v(i - 4 + HALF, q)
                for k in range(3, ROOT_STEPS):
                    root(k)
                if roots:
                    ch.need(ch.root)
                if live(i - 1):
                    wait(dve, b_keep, i - 1)
                    wait(dve, b_xt_ps, i - 1)
                    TT(halves(x1e), halves(wh), bc(ry[:, 0:NE], F), ALU.mult).then_inc(b_x1, 1)
                if live(i - 2):
                    dense_x1(i - 2 + HALF, q)
                if live(i - 5):
                    dense_out(i - 5 + HALF, 1 - q)
                if live(i):
                    wait(dve, b_pg[q], (h + 1) * (32 * G))
                    wait(dve, b_x1, i)
                    TT(wh[:, :, :], y_all[:, grp(i), :], xg[q][:, :, :], ALU.add).then_inc(b_v, 1)
                if live(i - 4):
                    dense_var2(i - 4 + HALF)
                if live(i):
                    wait(dve, b_sq, i + 1)
                    V.tensor_reduce(raw[:, 0:NE], halves(sq), AXX, ALU.add).then_inc(b_var, 1)
                if live(i - 1):
                    dense_var1(i - 1 + HALF)

            over_groups(dve, GROUPS, body_b, ch, B_STEPS)

            for done in b_acc:
                dve.wait_ge(done, 8 * T)
            ch = Chain(dve, c_chain)

            def body_c(i, q, h):
                if live(i - 1):
                    wait(dve, c_o_ps, i)
                    ch.step(TT(prod[:, :, :], p_z[:, 0:G * F].rearrange("p (g f) -> p g f", f=F),
                               bn2_c[:, :].unsqueeze(1).to_broadcast([P, G, F]), ALU.add))
                    TT(wh[:, :, 0:F], prod[:, :, :], y_all[:, grp(i - 1), 0:F], ALU.add).then_inc(c_v, 1)
                    wait(dve, c_srcb, i * 16)
                    TT(same[0][:, :, :], srcb[:, :, :], src_f[:, grp(i - 1)].unsqueeze(2).to_broadcast([P, G, P]),
                       ALU.is_equal).then_inc(c_eq, 1)
                    wait(dve, c_sq, i)
                    V.tensor_reduce(raw[:, 0:G], sq[:, :, 0:F], AXX, ALU.add).then_inc(c_var, 1)
                    wait(dve, c_var, i)
                    ch.need(variances(ch, slice(0, NE)))
                    rsqrt_step(ch, 0)
                    t = ch.mark(V.tensor_reduce(cnt[:, :], same[0][:, :, :], AXX, ALU.add))
                    rsqrt_step(ch, 1)
                    ch.need(t)
                    t = ch.mark(TS(cnt[:, :], cnt[:, :], 0.0, float(N), ALU.is_gt, ALU.mult))
                    rsqrt_step(ch, 2)
                    ch.need(t)
                    for done in c_sct:
                        wait(dve, done, (i - 2) * (8 * G))
                    TT(si[1 - q][:, :], cnt[:, :], sct_idx[:, grp(i - 1)], ALU.max).then_inc(c_idx, 1)
                    for k in range(3, ROOT_STEPS):
                        rsqrt_step(ch, k)
                    ch.need(ch.root)
                    TT(sm[1 - q][:, :, :], wh[:, :, 0:F], bc(ry[:, 0:G], F), ALU.mult).then_inc(c_out, 1)

            over_groups(dve, GROUPS, body_c, ch, C_STEPS)


_INS = ['x', 'src', 'dst', 'edge_attr_32', 'edge_weight', 'edge_weight_n2', 'L0_gnn_W', 'L0_gnn_b',
        'L0_gnn_deg_coeff', 'L0_gnn_coeff_param', 'L0_gnn_scale_param', 'L1_gnn_We1', 'L1_gnn_be1', 'L1_gnn_We2',
        'L1_gnn_be2', 'L1_gnn_Wn1', 'L1_gnn_bn1', 'L1_gnn_Wn2', 'L1_gnn_bn2']
_OUTS = [((100000, 64), 'float32')]


def kernel(**inputs):
    import numpy as _np
    import concourse.bacc as _bacc
    from concourse import mybir as _mybir
    from concourse.bass_utils import run_bass_kernel_spmd as _run

    nc = _bacc.Bacc("TRN2", target_bir_lowering=False, num_devices=1)
    arrays, args = {}, []
    for name in _INS:
        a = _np.ascontiguousarray(inputs[name])
        arrays[f"in_{name}_dram"] = a
        args.append(nc.dram_tensor(f"in_{name}_dram", a.shape, _mybir.dt.from_np(a.dtype), kind="ExternalInput").ap())
    for i, (shape, dtype) in enumerate(_OUTS):
        dt = _mybir.dt.from_np(_np.dtype(dtype))
        args.append(nc.dram_tensor(f"out_{i}_dram", shape, dt, kind="ExternalOutput").ap())
    gnn(nc, *args)
    r = _run(nc, [arrays], core_ids=[0])
    return r.results[0]["out_0_dram"]
```
